# Optimizing a Trainium2 kernel written in Bass

```python
import numpy as np
import jax
import jax.numpy as jnp

def _softmax(x, axis=-1):
    return jax.nn.softmax(x, axis=axis)

def _gelu(x):
    return jax.nn.gelu(x, approximate=True)

def _silu(x):
    return jax.nn.silu(x)

def _sigmoid(x):
    return jax.nn.sigmoid(x)

def _layernorm(x, axis=-1, eps=1e-05):
    m = jnp.mean(x, axis=axis, keepdims=True)
    v = jnp.var(x, axis=axis, keepdims=True)
    return (x - m) / jnp.sqrt(v + eps)

def _scatter_add(tgt, idx, src, axis=0):
    return tgt.at[idx].add(src)

def _segment_sum(src, seg, n):
    return jax.ops.segment_sum(src, seg, n)
kernel_name = 'mk_gnn_ffn_d1_gnn_r32_fc9f8d'

def setup_inputs(seed: int=0):
    np.random.seed(seed)
    _w = jnp.asarray

    def _rec_inputs():
        import jax
        import jax.numpy as jnp
        _gk = jax.random.key(seed)
        x = -0.000202 + 1 * jax.random.normal(jax.random.fold_in(_gk, 1), (3125, 256), jnp.float32)
        _s = jax.random.randint(jax.random.fold_in(_gk, 2), (25000,), 0, 3125, jnp.int32)
        _d = jax.random.randint(jax.random.fold_in(_gk, 3), (25000,), 0, 3125, jnp.int32)
        _loop = jnp.arange(3125, dtype=jnp.int32)
        src = jnp.concatenate([_s, _d, _loop])
        dst = jnp.concatenate([_d, _s, _loop])
        _o = jnp.argsort(dst, stable=True)
        src = src[_o]
        dst = dst[_o]
        edge_attr3_3x1 = 0.000555802 + 0.999374 * jax.random.normal(jax.random.fold_in(_gk, 12), (53125, 3, 1), jnp.float32)
        edge_attr3_5x1 = 0.0012042 + 1.00028 * jax.random.normal(jax.random.fold_in(_gk, 13), (53125, 5, 1), jnp.float32)
        edge_attr_64 = -8.62073e-06 + 0.999901 * jax.random.normal(jax.random.fold_in(_gk, 14), (53125, 64), jnp.float32)
        edge_weight1 = jax.random.uniform(jax.random.fold_in(_gk, 15), (53125, 1), jnp.float32, 0.0, 0.999998)
        return (x, src, dst, edge_attr3_3x1, edge_attr3_5x1, edge_attr_64, edge_weight1)
    x, src, dst, edge_attr3_3x1, edge_attr3_5x1, edge_attr_64, edge_weight1 = _rec_inputs()

    def _L0_gnn_setup():
        import jax, jax.numpy as jnp
        import numpy as np
        LN_EPS = 1e-05

        def _layernorm(x, g, b):
            m = jnp.mean(x, axis=-1, keepdims=True)
            v = jnp.var(x, axis=-1, keepdims=True)
            return (x - m) / jnp.sqrt(v + LN_EPS) * g + b
        key = jax.random.key(seed)
        ks = jax.random.split(key, 16)
        N, E, D, P = (25000, 15625, 256, 64)

        def rn(k, shape, scale=1.0):
            return jax.random.normal(k, shape, dtype=jnp.float32) * scale
        return {'x': rn(ks[0], (N, D)), 'rbf_r': rn(ks[1], (E, P)), 'factor_r': jax.random.uniform(ks[2], (E, 1), dtype=jnp.float32), 'sph_v0': rn(ks[3], (E, 5, 1)), 'sph_v1': rn(ks[4], (E, 3, 1)), 'W_down': rn(ks[5], (D, P), D ** (-0.5)), 'b_down': jnp.zeros((P,), jnp.float32), 'W_up0': rn(ks[6], (P, 2 * P), P ** (-0.5)), 'b_up0': jnp.zeros((2 * P,), jnp.float32), 'W_up1': rn(ks[7], (P, 2 * P), P ** (-0.5)), 'W_uph': rn(ks[8], (P, 2 * P), P ** (-0.5)), 'W_n1': rn(ks[9], (6 * P, D), (6 * P) ** (-0.5)), 'b_n1': jnp.zeros((D,), jnp.float32), 'ln_g': jnp.ones((D,), jnp.float32), 'ln_b': jnp.zeros((D,), jnp.float32), 'W_n2': rn(ks[10], (D, D), D ** (-0.5)), 'b_n2': jnp.zeros((D,), jnp.float32), 'j': jax.random.randint(ks[11], (E,), 0, N, dtype=jnp.int32), 'i': jax.random.randint(ks[12], (E,), 0, N, dtype=jnp.int32)}
    _L0_gnn_all = _L0_gnn_setup()
    _L0_gnn_in = {k: v for k, v in _L0_gnn_all.items() if k in ('W_down', 'b_down', 'W_up0', 'b_up0', 'W_up1', 'W_uph', 'W_n1', 'b_n1', 'ln_g', 'ln_b', 'W_n2', 'b_n2')}
    del _L0_gnn_all

    def _L0_ffn_setup():
        import jax, jax.numpy as jnp
        import numpy as np
        C = 256
        HID = 1024
        E = 8
        TEMP = 1.0
        key = jax.random.key(seed)
        ks = jax.random.split(key, 7)
        x = jax.random.normal(ks[0], (8, 512, C), dtype=jnp.float32)
        W1 = jax.random.normal(ks[1], (C, HID), dtype=jnp.float32) * 0.02
        b1 = jnp.zeros((HID,), dtype=jnp.float32)
        Wg = jax.random.normal(ks[2], (HID, E), dtype=jnp.float32) * 0.02
        bg = jnp.zeros((E,), dtype=jnp.float32)
        Wd = jax.random.normal(ks[3], (E, HID, C), dtype=jnp.float32) * 0.02
        bd = jnp.zeros((E, C), dtype=jnp.float32)
        return {'x': x, 'W1': W1, 'b1': b1, 'Wg': Wg, 'bg': bg, 'Wd': Wd, 'bd': bd}
    _L0_ffn_all = _L0_ffn_setup()
    _L0_ffn_in = {k: v for k, v in _L0_ffn_all.items() if k in ('W1', 'b1', 'Wg', 'bg', 'Wd', 'bd')}
    del _L0_ffn_all
    return {'x': x, 'src': src, 'dst': dst, 'edge_attr3_3x1': edge_attr3_3x1, 'edge_attr3_5x1': edge_attr3_5x1, 'edge_attr_64': edge_attr_64, 'edge_weight1': edge_weight1, 'L0_gnn_W_down': _L0_gnn_in['W_down'], 'L0_gnn_b_down': _L0_gnn_in['b_down'], 'L0_gnn_W_up0': _L0_gnn_in['W_up0'], 'L0_gnn_b_up0': _L0_gnn_in['b_up0'], 'L0_gnn_W_up1': _L0_gnn_in['W_up1'], 'L0_gnn_W_uph': _L0_gnn_in['W_uph'], 'L0_gnn_W_n1': _L0_gnn_in['W_n1'], 'L0_gnn_b_n1': _L0_gnn_in['b_n1'], 'L0_gnn_ln_g': _L0_gnn_in['ln_g'], 'L0_gnn_ln_b': _L0_gnn_in['ln_b'], 'L0_gnn_W_n2': _L0_gnn_in['W_n2'], 'L0_gnn_b_n2': _L0_gnn_in['b_n2'], 'L0_ffn_W1': _L0_ffn_in['W1'], 'L0_ffn_b1': _L0_ffn_in['b1'], 'L0_ffn_Wg': _L0_ffn_in['Wg'], 'L0_ffn_bg': _L0_ffn_in['bg'], 'L0_ffn_Wd': _L0_ffn_in['Wd'], 'L0_ffn_bd': _L0_ffn_in['bd']}

def reference(x, src, dst, edge_attr3_3x1, edge_attr3_5x1, edge_attr_64, edge_weight1, L0_gnn_W_down, L0_gnn_b_down, L0_gnn_W_up0, L0_gnn_b_up0, L0_gnn_W_up1, L0_gnn_W_uph, L0_gnn_W_n1, L0_gnn_b_n1, L0_gnn_ln_g, L0_gnn_ln_b, L0_gnn_W_n2, L0_gnn_b_n2, L0_ffn_W1, L0_ffn_b1, L0_ffn_Wg, L0_ffn_bg, L0_ffn_Wd, L0_ffn_bd):
    import jax
    import jax.numpy as jnp

    def _L0_gnn_ref(x, rbf_r, factor_r, sph_v0, sph_v1, W_down, b_down, W_up0, b_up0, W_up1, W_uph, W_n1, b_n1, ln_g, ln_b, W_n2, b_n2, j, i):
        import jax, jax.numpy as jnp
        import numpy as np
        LN_EPS = 1e-05

        def _layernorm(x, g, b):
            m = jnp.mean(x, axis=-1, keepdims=True)
            v = jnp.var(x, axis=-1, keepdims=True)
            return (x - m) / jnp.sqrt(v + LN_EPS) * g + b
        N = x.shape[0]
        _x = x @ W_down + b_down
        l0_pair = _x[j] * rbf_r * factor_r
        agg0 = jax.ops.segment_sum(l0_pair, i, num_segments=N)
        agg1 = jax.ops.segment_sum(l0_pair[:, None, :] * sph_v1, i, num_segments=N)
        aggh = jax.ops.segment_sum(l0_pair[:, None, :] * sph_v0, i, num_segments=N)
        l0_node = _x * agg0 @ W_up0 + b_up0
        l1_node = jnp.sum(jnp.square(_x[:, None, :] * agg1 @ W_up1), axis=1)
        lh_node = jnp.sum(jnp.square(_x[:, None, :] * aggh @ W_uph), axis=1)
        node = jnp.concatenate([l0_node, l1_node, lh_node], axis=-1)
        h = jax.nn.silu(_layernorm(node @ W_n1 + b_n1, ln_g, ln_b))
        return h @ W_n2 + b_n2 + x

    def _L0_ffn_ref(x, W1, b1, Wg, bg, Wd, bd):
        import jax, jax.numpy as jnp
        import numpy as np
        C = 256
        HID = 1024
        E = 8
        TEMP = 1.0
        orig_shape = x.shape
        xf = x.reshape(-1, orig_shape[-1])
        H = jax.nn.gelu(xf @ W1 + b1, approximate=False)
        probs = jax.nn.softmax((H @ Wg + bg) / TEMP, axis=-1)
        assign = jnp.argmax(probs, axis=-1)
        out = jnp.zeros_like(xf)
        for e in range(Wd.shape[0]):
            y = H @ Wd[e] + bd[e]
            sel = (assign == e)[:, None]
            out = out + jnp.where(sel, probs[:, e:e + 1] * y, 0.0)
        return out.reshape(orig_shape)
    x = x + _L0_gnn_ref(_layernorm(x, axis=-1), edge_attr_64, edge_weight1, edge_attr3_5x1, edge_attr3_3x1, L0_gnn_W_down, L0_gnn_b_down, L0_gnn_W_up0, L0_gnn_b_up0, L0_gnn_W_up1, L0_gnn_W_uph, L0_gnn_W_n1, L0_gnn_b_n1, L0_gnn_ln_g, L0_gnn_ln_b, L0_gnn_W_n2, L0_gnn_b_n2, dst, src)
    x = x + _L0_ffn_ref(_layernorm(x, axis=-1)[None], L0_ffn_W1, L0_ffn_b1, L0_ffn_Wg, L0_ffn_bg, L0_ffn_Wd, L0_ffn_bd)[0]
    return x

_drawn_inputs = setup_inputs


def setup_inputs(seed=0):
    import zlib

    import numpy as np

    out = dict(_drawn_inputs(seed))
    spreads = {'L0_gnn_b_down': (0.0, 0.1),
     'L0_gnn_b_up0': (0.0, 0.8),
     'L0_gnn_b_n1': (0.0, 0.8),
     'L0_gnn_ln_g': (1.0, 0.2),
     'L0_gnn_ln_b': (0.0, 0.284),
     'L0_gnn_b_n2': (0.0, 0.1),
     'L0_ffn_b1': (0.0, 0.8),
     'L0_ffn_bg': (0.0, 0.771),
     'L0_ffn_bd': (0.0, 0.8)}
    factors = {'L0_gnn_W_up0': 3.255, 'L0_ffn_W1': 5.499, 'L0_ffn_Wg': 6.137, 'L0_ffn_Wd': 6.776}
    for name, (base, spread) in spreads.items():
        noise = np.random.default_rng([zlib.crc32(name.encode()), seed]).standard_normal(out[name].shape)
        drawn = base * np.exp(spread * noise) if base else spread * noise
        out[name] = jnp.asarray(drawn.astype(out[name].dtype))
    for name, factor in factors.items():
        out[name] = (out[name] * factor).astype(out[name].dtype)
    return out
```

```python
import concourse.bass as bass
from concourse import mybir
from contextlib import ExitStack

F32 = mybir.dt.float32
BF16 = mybir.dt.bfloat16
I32 = mybir.dt.int32
ALU = mybir.AluOpType
ACT = mybir.ActivationFunctionType
AX = mybir.AxisListType

N, D, P, E = 3125, 256, 64, 53125
HID, NE = 1024, 8
S3, S5 = 3, 5
PLANES = 1 + S3 + S5
LN_EPS = 1e-5
L = 128
NT = -(-N // L)
N_FULL = N // L * L
N_TAIL = N - N_FULL
W = 32
NB = -(-N // W)
NK = NB + 1
PAIRS = NB // 2
SLOTS = 5
CAP = SLOTS * L
COLS = E // L
E_TAIL = E - COLS * L
TILES = COLS + 1
CHUNK = 16
CHUNKS = TILES // CHUNK
GRP = 4
REC = P + PLANES + 2
R_FAC, R_DST, R_LOC = P, P + PLANES, P + PLANES + 1
ROWS = NB * CAP
MREC = 2 * D + 2
MSLOTS = (N - NE) // L + NE
TAG = 4096
HALF = HID // L // 2
RING, XRING = 8, 4
AHEAD = 4
RSQRT = float(0x5f3759df)
ZCOLS = 525
WORK = 10632
BW = PLANES * W


def gnn_moe(nc, x, src, dst, sph_b, sph_a, rbf, fac, w_down, b_down, w_up0, b_up0, w_up1, w_uph,
            w_n1, b_n1, ln_g, ln_b, w_n2, b_n2, w1, b1, wg, bg, wd, bd, out):
    ctx = ExitStack()
    with ctx:
        def sb(name, shape, dt=F32):
            return ctx.enter_context(nc.sbuf_tensor(name, shape, dt))

        def sem(name):
            return ctx.enter_context(nc.semaphore(name))

        table = nc.dram_tensor("pair_table", [NT * L, P], F32, kind="Internal").ap()
        srt = nc.dram_tensor("sorted_edges", [ROWS, REC], F32, kind="Internal").ap()
        msrt = nc.dram_tensor("sorted_tokens", [(MSLOTS + 1) * L, MREC], F32, kind="Internal").ap()

        recs = sb("recs", [L, NT, MREC])
        hid = recs[:, :, 0:D]
        res = recs[:, :, D:2 * D]
        arena = sb("arena", [L, 20800])
        work = sb("work", [L, WORK])
        onehot = arena[:, 0:(TILES + GRP) * NK // 2].bitcast(BF16).rearrange("p (t k) -> p t k", k=NK)
        agg = arena[:, 0:(PAIRS + 1) * BW].rearrange("p (q s w) -> p q s w", s=PLANES, w=W)
        at = (PAIRS + 1) * BW
        ring = []
        for n in range(RING):
            ring.append(arena[:, at:at + SLOTS * REC].rearrange("p (s r) -> p s r", r=REC))
            at += SLOTS * REC
        xg = []
        for n in range(XRING):
            xg.append(arena[:, at:at + SLOTS * P].rearrange("p (s c) -> p s c", c=P))
            at += SLOTS * P
        pair = []
        for n in range(2):
            pair.append(arena[:, at:at + SLOTS * P].rearrange("p (s c) -> p s c", c=P))
            at += SLOTS * P
        oh5 = []
        for n in range(2):
            oh5.append(arena[:, at:at + SLOTS * W].rearrange("p (s w) -> p s w", w=W))
            at += SLOTS * W
        assert at <= 20800
        wd_sb = arena[:, 0:NE * HID // L * D]
        bd_sb = arena[0:1, 18432:18432 + NE * D]
        at = 0

        def take(n):
            nonlocal at
            at += n
            return work[:, at - n:at]

        sph3 = take(TILES * S3).rearrange("p (t s) -> p t s", s=S3)
        sph5 = take(TILES * S5).rearrange("p (t s) -> p t s", s=S5)
        facs = take(TILES)
        dstf = take(TILES)
        locf = take(TILES)
        keyf = take(TILES)
        srci = take(TILES).bitcast(I32)
        dsti = take(TILES).bitcast(I32)
        keyb = take(TILES // 2).bitcast(BF16)
        at_rec = at
        rec = [take(CHUNK * REC).rearrange("p (t r) -> p t r", r=REC) for _ in range(2)]
        tab = take(NT * P).rearrange("p (t c) -> p t c", c=P)
        prod = work[:, at - NT * P:at - NT * P + CHUNK * NK].rearrange("p (t k) -> p t k", k=NK)
        assert at <= WORK
        xn = [hid[:, n, :] for n in range(2)]
        xnt = [hid[:, 2 + n, :].rearrange("p (k n) -> p k n", k=2) for n in range(2)]
        base4 = hid[0:1, 4:4 + GRP, 0:NK]
        at = 0
        nx = [take(2 * BW) for _ in range(2)]
        sq = [take(2 * 8 * 2 * W).rearrange("p (h s n) -> p h s n", h=2, s=8) for _ in range(2)]
        at_node = at
        node = [take(3 * L).rearrange("p (k q h w) -> p k q h w", k=3, q=2, h=2) for _ in range(2)]
        u = [take(D) for _ in range(2)]
        xf = [take(D) for _ in range(2)]
        hs = [take(D) for _ in range(2)]
        ht = [take(D).rearrange("p (k n) -> p k n", k=2) for _ in range(2)]
        hx = [take(D).rearrange("p (k n) -> p k n", k=2) for _ in range(2)]
        hh = [take(HID).rearrange("p (j n) -> p j n", j=HID // L) for _ in range(1)] * 2
        at_ohs = at
        assert at_ohs >= at_rec
        ohs = [take(SLOTS * BW).rearrange("p (s k w) -> p s k w", k=PLANES, w=W) for _ in range(2)]
        lg = take(NT * NE).rearrange("p (t e) -> p t e", e=NE)
        assert at <= WORK
        at = at_ohs
        mr = [take(MREC) for _ in range(4)]
        yo = [take(D) for _ in range(2)]
        assert at <= WORK - NT * NE
        at = 0
        le = take(NT * NE).rearrange("p (t e) -> p t e", e=NE)
        ohx, cum, sel = (take((NE + 1) * NT).rearrange("p (e t) -> p e t", t=NT) for _ in range(3))
        zer = take((NE + 1) * NT)
        kcm = take(MSLOTS * NE).rearrange("p (k e) -> p k e", e=NE)
        tix, eix, pad, mpos = (take(NT) for _ in range(4))
        cnt, slf, csl, off = (take(NE + 1) for _ in range(4))
        kex = take(MSLOTS)
        cni, kei, mpi = (take(n).bitcast(I32) for n in (NE + 1, MSLOTS, NT))
        assert at <= at_node
        hh2 = [hh[0], work[:, at:at + HID].rearrange("p (j n) -> p j n", j=HID // L)]
        assert at + HID <= at_node
        at = (PAIRS + 1) * BW

        def tail(n):
            nonlocal at
            at += n
            return arena[:, at - n:at]

        sp_rbf, sp_x, sp_pair = tail(P), tail(P), tail(P)
        sp_fac = tail(PLANES)
        sp_oh = tail(W)
        sp_key = [tail(W) for _ in range(2)]
        sp_ohs = [tail(BW).rearrange("p (k w) -> p k w", w=W) for _ in range(2)]

        zeros = sb("zeros", [L, ZCOLS])
        xT = sb("xT", [L, PAIRS + 1, W])
        ident = sb("ident", [L, L])
        onesf = sb("onesf", [L, L])
        lowf = sb("lowf", [L, L])
        lowb = sb("lowb", [L, L], BF16)
        uppb = sb("uppb", [L, L], BF16)
        onesb = sb("onesb", [L, L], BF16)
        keys = sb("keys", [L, NK], BF16)
        keysf = sb("keysf", [L, NK])
        iota_w = sb("iota_w", [L, W])
        wdn = sb("wdn", [L, 2, P])
        bdn_row = sb("bdn_row", [1, P])
        bdn_col = sb("bdn_col", [L, 1])
        wup = sb("wup", [L, 3, L])
        bup = sb("bup", [L, 1])
        wn1 = sb("wn1", [L, 3, D])
        bn1 = sb("bn1", [L, D])
        gam = sb("gam", [L, D])
        bet = sb("bet", [L, D])
        wn2 = sb("wn2", [L, 2, D])
        bn2 = sb("bn2", [L, D])
        b1c = sb("b1c", [L, HID // L])
        w1_sb = sb("w1_sb", [L, 2, HID])
        wgs = sb("wgs", [L, HID // L, NE])
        bgr = sb("bgr", [L, NE])
        st = [sb(f"st{n}", [L, 6]) for n in range(2)]
        mv = [sb(f"mv{n}", [L, 2]) for n in range(2)]
        mvs = sb("mvs", [L, NT, 2])
        vv = sb("vv", [L, NT])
        v1 = [sb(f"v1_{k}", [L, 1]) for k in range(2)]
        r1 = [sb(f"r1_{k}", [L, 1]) for k in range(2)]
        a1 = [sb(f"a1_{k}", [L, 1]) for k in range(2)]
        mxo = sb("mxo", [L, 1])
        spill = sb("spill", [1, 1], I32)
        sp_eq = [sb(f"sp_eq{n}", [L, 1]) for n in range(2)]
        sp_idx = sb("sp_idx", [L, 1], I32)
        rs = sb("rs", [L, NT])
        ra = sb("ra", [L, NT])
        posf = sb("posf", [L, CHUNK])
        rnk = sb("rnk", [L, CHUNK])
        ovr = sb("ovr", [L, TILES])
        posi = [sb(f"posi{n}", [L, CHUNK], I32) for n in range(2)]
        gidx = [sb(f"gidx{n}", [L, SLOTS], I32) for n in range(RING)]
        m1 = sb("m1", [L, NT])
        tok = sb("tok", [L, NT])
        e9 = sb("e9", [L, NE + 1])
        kio = sb("kio", [L, MSLOTS])
        oix = [sb(f"oix{n}", [L, 1], I32) for n in range(4)]

        ps = [ctx.enter_context(nc.psum_tensor(f"bank{n}", [L, 512], F32)) for n in range(8)]

        names = """turns ld_idx ld_tail ld_x ld_edge ld_w ld_late zfill zfill_m msets consts tbl_out v
            xn_ready xn_read xt_sb pr_ps pr_sb
            oh_ready rank_done rank_read base_ready flds_v flds_a pos_ready sum_in sum_ps spill_set
            g_ready oh_w pair_ready ohs_ready agg_ps agg_sb
            nx_ready up_ps up_sb red_sb n1_ps n1_read hn_v sil_in sil_out th_ps th_sb y_ps y_read y_v
            xf_ready tx_ps tx_sb h_ps h_sb g_ps g_read
            ex_in ex_out ohx_ready rk_ps moe_rdy tok_out
            mt_ps mt_sb mh_ps mh_sb my_ps my_sb
            sp_ld sp_ix sp_gx sp_v sp_in sp_ps sp_add sp_a sp_b""".split()
        s = {n: sem(n) for n in names}
        ld_rec = [sem(f"ld_rec{n}") for n in range(2)]
        scat = [sem(f"scat{n}") for n in range(2)]
        ld_ring = [sem(f"ld_ring{n}") for n in range(RING)]
        gath = [sem(f"gath{n}") for n in range(XRING)]
        ld_mr = [sem(f"ld_mr{n}") for n in range(4)]
        wr_y = [sem(f"wr_y{n}") for n in range(2)]

        def wait_apart(eng, sm, value):
            eng.wait_ge(sm, value)
            eng.sem_inc(s["turns"], 1)

        def main_cols(a):
            return a[0:COLS * L].rearrange("(p c) -> p c", p=L)

        def tiles(eng, n, body):
            with eng.Fori(0, n // 2) as i:
                body(2 * i, 0)
                body(2 * i + 1, 1)
            if n % 2:
                body(n - 1, 0)

        def buckets(eng, body):
            whole = (NB - AHEAD) // RING
            with eng.Fori(0, whole) as i:
                for j in range(RING):
                    body(i, j)
            for b in range(whole * RING, NB):
                body(b // RING, b % RING)

        def stages(eng, bucket, stage):
            def step(i, half):
                loop = not isinstance(i, int)
                for q in range(4):
                    if loop or 4 * (2 * i + half) + q < NB:
                        bucket(i, 4 * half + q)
                    for lag, run in stage[q]:
                        if loop or 0 <= 2 * i + half - lag < NT:
                            run(2 * i + half - lag, (half - lag) % 2)

            for n_ in range(4):
                step(n_ // 2, n_ % 2)
            with eng.Fori(2, (NB - AHEAD) // RING) as i:
                step(i, 0)
                step(i, 1)
            for n_ in range((NB - AHEAD) // RING * 2, NT + 4):
                step(n_ // 2, n_ % 2)

        def choose(eng, fused, apart):
            eng.wait_ge(s["spill_set"], 1)
            full = eng.value_load(spill[0:1, 0:1], min_val=0, max_val=1)
            with eng.If(full):
                apart()
            with eng.Else():
                fused()

        block = ctx.enter_context(nc.Block())

        @block.sync
        def _(sp):
            sp.dma_start(srci[:, 0:COLS], main_cols(src)).then_inc(s["ld_idx"], 16)
            sp.dma_start(dsti[:, 0:COLS], main_cols(dst)).then_inc(s["ld_idx"], 16)
            sp.dma_start(res[:, 0:NT - 1, :], x[0:N_FULL, :].rearrange("(t p) d -> p t d", p=L)).then_inc(s["ld_x"], 16)
            sp.wait_ge(s["msets"], 1)
            sp.dma_start(srci[0:E_TAIL, COLS:TILES], src[COLS * L:E].unsqueeze(1)).then_inc(s["ld_tail"], 16)
            sp.dma_start(dsti[0:E_TAIL, COLS:TILES], dst[COLS * L:E].unsqueeze(1)).then_inc(s["ld_tail"], 16)
            sp.dma_start(res[0:N_TAIL, NT - 1, :], x[N_FULL:N, :]).then_inc(s["ld_x"], 16)
            sp.dma_start(facs[:, 0:COLS], fac[0:COLS * L, :].rearrange("(p c) a -> p (c a)", p=L)).then_inc(s["ld_edge"], 16)
            sp.dma_start(sph3[:, 0:COLS, :], sph_a[0:COLS * L].rearrange("(p c) s a -> p c (s a)", p=L)).then_inc(s["ld_edge"], 16)
            sp.dma_start(sph5[:, 0:COLS, :], sph_b[0:COLS * L].rearrange("(p c) s a -> p c (s a)", p=L)).then_inc(s["ld_edge"], 16)
            sp.dma_start(facs[0:E_TAIL, COLS:TILES], fac[COLS * L:E, :]).then_inc(s["ld_edge"], 16)
            sp.dma_start(sph3[0:E_TAIL, COLS, :], sph_a[COLS * L:E].rearrange("p s a -> p (s a)")).then_inc(s["ld_edge"], 16)
            sp.dma_start(sph5[0:E_TAIL, COLS, :], sph_b[COLS * L:E].rearrange("p s a -> p (s a)")).then_inc(s["ld_edge"], 16)

            def load_chunk(i, par, c0, first=False, last=False):
                if not first:
                    sp.wait_ge(scat[par], CHUNK * 16 * i)
                rows = rbf[0:COLS * L, :].rearrange("(p c) f -> p c f", p=L)
                sp.dma_start(rec[par][:, 0:CHUNK - 1, 0:P], rows[:, bass.ds(c0, CHUNK - 1), :]).then_inc(ld_rec[par], 16)
                if last:
                    sp.dma_start(rec[par][0:E_TAIL, CHUNK - 1, 0:P], rbf[COLS * L:E, :]).then_inc(ld_rec[par], 16)
                else:
                    sp.dma_start(rec[par][:, CHUNK - 1:CHUNK, 0:P], rows[:, bass.ds(c0 + CHUNK - 1, 1), :]).then_inc(ld_rec[par], 16)

            load_chunk(0, 0, 0, first=True)
            load_chunk(0, 1, CHUNK, first=True)
            with sp.Fori(1, CHUNKS // 2 - 1) as i:
                load_chunk(i, 0, i * (2 * CHUNK))
                load_chunk(i, 1, i * (2 * CHUNK) + CHUNK)
            end = CHUNKS // 2 - 1
            load_chunk(end, 0, end * 2 * CHUNK)
            load_chunk(end, 1, end * 2 * CHUNK + CHUNK, last=True)

            for par in range(2):
                sp.wait_ge(scat[par], CHUNK * 16 * (CHUNKS // 2))
            by_bucket = srt.rearrange("(b p s) r -> b p s r", b=NB, s=SLOTS)

            def load_bucket(i, j):
                sp.wait_ge(s["pair_ready"], i * RING + j + 1)
                sp.dma_start(ring[j], by_bucket[bass.ds(i * RING + j, 1), :, :, :].rearrange("b p s r -> (b p) s r")).then_inc(ld_ring[j], 16)

            def spill_rows(c, tail=False):
                if not (isinstance(c, int) and c == 0):
                    sp.wait_ge(s["sp_v"], 3 * c)
                if tail:
                    sp.dma_start(sp_rbf[0:E_TAIL, :], rbf[COLS * L:E, :]).then_inc(s["sp_ld"], 16)
                else:
                    rows = rbf[0:COLS * L, :].rearrange("(p c) f -> p c f", p=L)
                    sp.dma_start(sp_rbf, rows[:, bass.ds(c, 1), :].rearrange("p c f -> p (c f)")).then_inc(s["sp_ld"], 16)

            def apart():
                buckets(sp, load_bucket)
                sp.wait_ge(s["pair_ready"], NB + RING)
                spill_rows(0)
                with sp.Fori(1, COLS) as c:
                    spill_rows(c)
                spill_rows(COLS, tail=True)

            choose(sp, lambda: buckets(sp, load_bucket), apart)
            sp.wait_ge(s["pair_ready"], NB + RING)
            sp.wait_ge(s["nx_ready"], NT)
            sp.dma_start(bd_sb, bd.rearrange("(a e) d -> a (e d)", a=1)).then_inc(s["ld_late"], 16)
            for e in range(NE):
                sp.dma_start(wd_sb.rearrange("p (e j d) -> p e j d", e=NE, j=HID // L)[:, e, :, :],
                             wd[e, :, :].rearrange("(j p) d -> p j d", p=L)).then_inc(s["ld_late"], 16)
            sp.wait_ge(s["tok_out"], 16 * NT)
            with sp.Fori(0, MSLOTS // 4) as i:
                for j in range(4):
                    sp.wait_ge(s["my_sb"], i * 4 + j + 1)
                    sp.dma_start(mr[j][:, :], msrt[bass.ds((i * 4 + j) * L, L), :]).then_inc(ld_mr[j], 16)

        @block.gpsimd
        def _(gp):
            gp.iota(keysf[:, :], pattern=[[1, NK]], base=0, channel_multiplier=0, allow_small_or_imprecise_dtypes=True).then_inc(s["consts"], 1)
            gp.iota(iota_w[:, :], pattern=[[1, W]], base=0, channel_multiplier=0, allow_small_or_imprecise_dtypes=True).then_inc(s["consts"], 1)
            gp.iota(e9[:, :], pattern=[[1, NE + 1]], base=0, channel_multiplier=0, allow_small_or_imprecise_dtypes=True).then_inc(s["consts"], 1)
            gp.iota(kio[:, :], pattern=[[1, MSLOTS]], base=0, channel_multiplier=0, allow_small_or_imprecise_dtypes=True).then_inc(s["consts"], 1)
            gp.iota(tok[:, :], pattern=[[L, NT]], base=0, channel_multiplier=1, allow_small_or_imprecise_dtypes=True).then_inc(s["consts"], 1)
            gp.memset(onesf[:, :], 1.0).then_inc(s["consts"], 1)
            gp.memset(ident[:, :], 0.0).then_inc(s["consts"], 1)
            gp.wait_ge(s["consts"], 7)
            gp.affine_select(out=ident[:, :], in_=ident[:, :], compare_op=ALU.not_equal, fill=1.0, base=0,
                             pattern=[[-1, L]], channel_multiplier=1).then_inc(s["consts"], 1)
            gp.affine_select(out=lowf[:, :], in_=onesf[:, :], compare_op=ALU.is_gt, fill=0.0, base=0,
                             pattern=[[1, L]], channel_multiplier=-1).then_inc(s["consts"], 1)
            gp.wait_ge(s["consts"], 9)
            gp.wait_ge(s["zfill"], 16)

            def scatter_chunk(i, par):
                wait_apart(gp, ld_rec[par], 32 * (i + 1))
                wait_apart(gp, s["flds_v"], 2 * i + par + 1)
                wait_apart(gp, s["flds_a"], 2 * i + par + 1)
                wait_apart(gp, s["pos_ready"], 2 * i + par + 1)
                for c in range(CHUNK):
                    gp.indirect_dma_start(out=srt[:, :], out_offset=bass.IndirectOffsetOnAxis(ap=posi[par][:, c:c + 1], axis=0),
                                          in_=rec[par][:, c, :], in_offset=None, bounds_check=ROWS - 1,
                                          oob_is_err=False).then_inc(scat[par], 16)

            with gp.Fori(0, CHUNKS // 2) as i:
                scatter_chunk(i, 0)
                scatter_chunk(i, 1)
            def gather(i, j):
                x_ = j % XRING
                wait_apart(gp, s["g_ready"], i * RING + j + 1)
                wait_apart(gp, s["pair_ready"], i * RING + j + 1 + RING - XRING)
                for c in range(SLOTS):
                    gp.indirect_dma_start(out=xg[x_][:, c, :], out_offset=None, in_=table[:, :],
                                          in_offset=bass.IndirectOffsetOnAxis(ap=gidx[j][:, c:c + 1], axis=0)).then_inc(gath[x_], 16)

            def spill_gather(c):
                wait_apart(gp, s["sp_ix"], c + 1)
                gp.indirect_dma_start(out=sp_x, out_offset=None, in_=table[:, :],
                                      in_offset=bass.IndirectOffsetOnAxis(ap=sp_idx[:, 0:1], axis=0)).then_inc(s["sp_gx"], 16)

            def apart():
                buckets(gp, gather)
                with gp.Fori(0, TILES) as c:
                    spill_gather(c)

            gp.wait_ge(s["tbl_out"], 16)
            choose(gp, lambda: buckets(gp, gather), apart)
            gp.wait_ge(s["zfill_m"], 16)
            gp.wait_ge(s["moe_rdy"], 1)
            for t in range(NT):
                gp.indirect_dma_start(out=msrt[:, :], out_offset=bass.IndirectOffsetOnAxis(ap=mpi[:, t:t + 1], axis=0),
                                      in_=recs[:, t, :], in_offset=None).then_inc(s["tok_out"], 16)
            with gp.Fori(0, MSLOTS // 4) as i:
                for j in range(4):
                    wait_apart(gp, s["my_sb"], i * 4 + j + 1 + 4)
                    gp.indirect_dma_start(out=out[:, :], out_offset=bass.IndirectOffsetOnAxis(ap=oix[j][:, 0:1], axis=0),
                                          in_=yo[j % 2][:, :], in_offset=None, bounds_check=N - 1,
                                          oob_is_err=False).then_inc(wr_y[j % 2], 16)
            for par in range(2):
                gp.wait_ge(wr_y[par], 16 * MSLOTS // 2)

        @block.scalar
        def _(act):
            loads = [(wdn[:, :, :], w_down.rearrange("(k p) c -> p k c", p=L)),
                     (bdn_row[:, :], b_down.unsqueeze(0)),
                     (bdn_col[0:P, :], b_down.unsqueeze(1)), (bdn_col[P:L, :], b_down.unsqueeze(1)),
                     (bup[:, :], b_up0.unsqueeze(1)),
                     (wn1[:, :, :], w_n1.rearrange("(k p) c -> p k c", p=L)), (bn1[:, :], b_n1.unsqueeze(0).broadcast_to([L, D])),
                     (gam[:, :], ln_g.unsqueeze(0).broadcast_to([L, D])), (bet[:, :], ln_b.unsqueeze(0).broadcast_to([L, D])),
                     (wn2[:, :, :], w_n2.rearrange("(k p) c -> p k c", p=L)), (bn2[:, :], b_n2.unsqueeze(0).broadcast_to([L, D])),
                     (wgs[:, :, :], wg.rearrange("(j p) e -> p j e", p=L)), (bgr[:, :], bg.unsqueeze(0).broadcast_to([L, NE]))]
            for h in range(2):
                for k, m in enumerate((w_up0, w_up1, w_uph)):
                    loads.append((wup[h * P:(h + 1) * P, k, :], m))
            for o, a in loads:
                act.dma_start(o, a).then_inc(s["ld_w"], 16)
            act.dma_start(b1c[:, :], b1.rearrange("(j p) -> p j", p=L), allow_slow_non_contiguous=True).then_inc(s["ld_w"], 16)
            act.dma_start(w1_sb[:, :, :], w1.rearrange("(k p) h -> p k h", p=L)).then_inc(s["ld_w"], 16)
            act.wait_ge(s["msets"], 1)
            rep = ROWS * REC // L // ZCOLS
            act.dma_start(srt.rearrange("(p a) r -> p (a r)", p=L).rearrange("p (n c) -> p n c", c=ZCOLS),
                          zeros[:, :].unsqueeze(1).broadcast_to([L, rep, ZCOLS])).then_inc(s["zfill"], 16)
            act.wait_ge(s["ld_w"], 16 * (len(loads) + 2))

            for n_, k in (("xt_sb", 2), ("pr_sb", 2), ("agg_sb", 2), ("up_sb", 2), ("sil_out", 2), ("th_sb", 1), ("tx_sb", 1),
                          ("h_sb", 2), ("mt_sb", 2), ("mh_sb", 2)):
                act.sem_inc(s[n_], k)

            def proj(t, par):
                act.wait_ge(s["xn_read"], t + 1 + 2)
                act.activation(xnt[par], ps[par][:, 0:D].rearrange("p (k n) -> p k n", k=2), ACT.Copy).then_inc(s["xt_sb"], 1)
                act.wait_ge(s["pr_ps"], t + 1)
                act.activation(tab[:, bass.ds(t, 1), :], ps[2 + par][:, 0:P].unsqueeze(1), ACT.Copy)
                for h in range(2):
                    rows = slice(h * P, (h + 1) * P)
                    done = act.activation(xT[rows, bass.ds(2 * t, 2), :],
                                          ps[4 + 2 * par + h][rows, 0:2 * W].rearrange("p (q w) -> p q w", q=2),
                                          ACT.Identity, bias=bdn_col[rows, :])
                done.then_inc(s["pr_sb"], 1)

            tiles(act, NT, proj)
            act.wait_ge(s["pr_sb"], NT + 2)
            act.dma_start(table.rearrange("(t p) c -> p t c", p=L), tab).then_inc(s["tbl_out"], 16)

            act.dma_start(msrt.rearrange("(p a) r -> p (a r)", p=L).rearrange("p (n c) -> p n c", c=MREC // 2),
                          zeros[:, 0:MREC // 2].unsqueeze(1).broadcast_to([L, 2 * (MSLOTS + 1), MREC // 2])).then_inc(s["zfill_m"], 16)

            def fields(i, par, first=False):
                c0 = i * (2 * CHUNK) + par * CHUNK
                if not first:
                    act.wait_ge(scat[par], CHUNK * 16 * i)
                for at_, a in ((R_FAC, facs), (R_DST, dstf), (R_LOC, locf)):
                    done = act.activation(rec[par][:, :, at_:at_ + 1], a[:, bass.ds(c0, CHUNK)].unsqueeze(2), ACT.Copy)
                done.then_inc(s["flds_a"], 1)

            act.wait_ge(s["msets"], 2)
            act.wait_ge(s["ld_edge"], 16 * 6)
            fields(0, 0, first=True)
            fields(0, 1, first=True)
            with act.Fori(1, CHUNKS // 2) as i:
                fields(i, 0)
                fields(i, 1)

            def indices(i, j):
                act.wait_ge(ld_ring[j], 16 * i + 16)
                act.wait_ge(s["pair_ready"], i * RING + j + 1)
                act.activation(gidx[j][:, :], ring[j][:, :, R_DST], ACT.Copy).then_inc(s["g_ready"], 1)

            def take_sums(i, j):
                ahead = j + AHEAD
                if not isinstance(i, int) or i * RING + ahead < NB:
                    indices(i + ahead // RING, ahead % RING)
                rows = slice(j % 2 * P, (j % 2 + 1) * P)
                act.wait_ge(s["agg_ps"], i * RING + j + 1 + 2)
                act.activation(agg[rows, bass.ds(i * (RING // 2) + j // 2, 1), :, :].rearrange("p q s w -> p (q s w)"),
                               ps[0][rows, 0:BW], ACT.Copy).then_inc(s["agg_sb"], 1)

            def squares(h):
                def run(t, par):
                    act.wait_ge(s["up_ps"], 2 * t + h + 1 + 4)
                    act.wait_ge(s["n1_ps"], t + 1)
                    act.activation(node[par][:, 0, :, h, :], ps[1][:, 0:2 * W].rearrange("p (q w) -> p q w", q=2),
                                   ACT.Identity, bias=bup[:, :])
                    act.activation(sq[par][:, h, 0:S3, :], ps[1][:, 2 * W:2 * W * (1 + S3)].rearrange("p (s n) -> p s n", s=S3), ACT.Square)
                    act.activation(sq[par][:, h, S3:S3 + S5, :], ps[2][:, 0:2 * W * S5].rearrange("p (s n) -> p s n", s=S5),
                                   ACT.Square).then_inc(s["up_sb"], 1)
                return run

            def silu(t, par):
                act.wait_ge(s["sil_in"], t + 1)
                act.wait_ge(s["th_ps"], t + 1)
                act.activation(hs[par], u[par], ACT.Silu).then_inc(s["sil_out"], 1)

            def turned_h(t, par):
                act.wait_ge(s["th_ps"], t + 1 + 2)
                act.activation(ht[par], ps[5][:, 0:D].rearrange("p (k n) -> p k n", k=2), ACT.Copy).then_inc(s["th_sb"], 1)

            def turned_x(t, par):
                act.wait_ge(s["tx_ps"], t + 1 + 2)
                act.activation(hx[par], ps[5][:, 0:D].rearrange("p (k n) -> p k n", k=2), ACT.Copy).then_inc(s["tx_sb"], 1)

            def gelus(bank, out_, lo):
                for m in range(HALF):
                    done = act.activation(out_[:, lo + m, :], ps[bank][:, m * L:(m + 1) * L], ACT.Gelu, bias=b1c[:, lo + m:lo + m + 1])
                return done

            def gelu(h):
                def run(t, par):
                    act.wait_ge(s["h_ps"], 2 * t + h + 1)
                    act.wait_ge(s["g_ps"], t + 1)
                    gelus(6 + h, hh[0], h * HALF).then_inc(s["h_sb"], 1)
                return run

            def fused():
                stages(act, take_sums, (((1, squares(0)), (2, turned_h), (3, gelu(0))), ((1, squares(1)),),
                                        ((3, gelu(1)),), ((2, turned_x), (1, silu))))

            def apart():
                buckets(act, take_sums)
                act.wait_ge(s["sp_add"], TILES * PAIRS)

                def tile(t, par):
                    for run in (squares(0), squares(1), silu, turned_h, turned_x, gelu(0), gelu(1)):
                        run(t, par)

                tiles(act, NT, tile)

            for j in range(AHEAD):
                indices(0, j)
            choose(act, fused, apart)
            act.wait_ge(s["ex_in"], 1)
            act.activation(le[:, :, :], le[:, :, :], ACT.Exp).then_inc(s["ex_out"], 1)

            def turned_m(t, par):
                act.wait_ge(s["mt_ps"], t + 1)
                act.activation(ht[par], ps[par][:, 0:D].rearrange("p (k n) -> p k n", k=2), ACT.Copy).then_inc(s["mt_sb"], 1)

            def gelu_m(t, par):
                act.wait_ge(s["mh_ps"], t + 1)
                act.wait_ge(s["my_ps"], t + 1)
                gelus(2 + 2 * par, hh2[par], 0)
                gelus(3 + 2 * par, hh2[par], HALF).then_inc(s["mh_sb"], 1)

            def both_m(t, par):
                turned_m(t + 1, 1 - par)
                gelu_m(t, par)

            turned_m(0, 0)
            tiles(act, MSLOTS - 2, both_m)
            both_m(MSLOTS - 2, 0)
            gelu_m(MSLOTS - 1, 1)

        @block.tensor
        def _(pe):
            for n_, k in (("xn_read", 2), ("agg_ps", 2), ("up_ps", 4), ("n1_ps", 2), ("th_ps", 2), ("tx_ps", 2), ("g_ps", 1), ("my_ps", 2)):
                pe.sem_inc(s[n_], k)
            pe.wait_ge(s["consts"], 9)
            pe.wait_ge(s["ld_w"], 16 * 21)

            def turn(src_, par):
                for k in range(2):
                    done = nc.tensor.transpose(ps[par][:, k * L:(k + 1) * L], src_[:, k * L:(k + 1) * L], ident[:, :])
                return done

            def proj(t, par):
                pe.wait_ge(s["xn_ready"], t + 1)
                pe.wait_ge(s["xt_sb"], t + 1)
                turn(xn[par], par).then_inc(s["xn_read"], 1)
                pe.wait_ge(s["xt_sb"], t + 1 + 2)
                pe.wait_ge(s["pr_sb"], t + 1)
                for k in range(2):
                    nc.tensor.matmul(ps[2 + par][:, 0:P], xnt[par][:, k, :], wdn[:, k, :], start=(k == 0), stop=False)
                nc.tensor.matmul(ps[2 + par][:, 0:P], onesf[0:1, :], bdn_row[:, :], start=False, stop=True)
                for h in range(2):
                    for k in range(2):
                        done = nc.tensor.matmul(ps[4 + 2 * par + h][h * P:(h + 1) * P, 0:2 * W], wdn[:, k, :],
                                                xnt[par][:, k, :].rearrange("p (q h w) -> p h q w", q=2, h=2)[:, h, :, :],
                                                start=(k == 0), stop=(k == 1))
                done.then_inc(s["pr_ps"], 1)

            tiles(pe, NT, proj)

            rank = ps[0][:, 0:GRP * NK]
            pe.wait_ge(s["base_ready"], 1)
            pe.wait_ge(s["pr_sb"], NT + 2)
            nc.tensor.matmul(rank, onesf[0:1, :], base4, start=True, stop=True)

            def ranks(i, par):
                for q in range(CHUNK // GRP):
                    g = i * (CHUNK // GRP) + q
                    if q == 0:
                        pe.wait_ge(s["oh_ready"], i + 1)
                    pe.wait_ge(s["rank_read"], g + 1)
                    for n_, m in ((0, uppb), (1, onesb), (2, onesb), (3, onesb), (4, lowb)):
                        done = nc.tensor.matmul(rank, m[:, :], onehot[:, bass.ds(g * GRP + n_, GRP), :].rearrange("p t k -> p (t k)"),
                                                start=False, stop=True, skip_group_check=True)
                    done.then_inc(s["rank_done"], 1)

            tiles(pe, CHUNKS, ranks)

            pe.wait_ge(s["sum_in"], 1)
            nc.tensor.matmul(ps[7][:, 0:1], onesf[:, :], mxo[:, :], start=True, stop=True).then_inc(s["sum_ps"], 1)

            def sums(i, j):
                o, b = j % 2, i * RING + j
                pe.wait_ge(s["pair_ready"], b + 1 + RING)
                pe.wait_ge(s["ohs_ready"], b + 1 + 2)
                pe.wait_ge(s["agg_sb"], b + 1)
                for c in range(SLOTS):
                    done = nc.tensor.matmul(ps[0][o * P:(o + 1) * P, 0:BW], pair[o][:, c, :],
                                            ohs[o][:, c, :, :].rearrange("p k w -> p (k w)"), start=(c == 0), stop=(c == SLOTS - 1))
                done.then_inc(s["agg_ps"], 1)

            def up(h):
                def run(t, par):
                    pe.wait_ge(s["nx_ready"], t + 1)
                    pe.wait_ge(s["up_sb"], 2 * t + h + 2)
                    rows = slice(h * P, (h + 1) * P)
                    for bank, lo, k, a, n_ in ((1, 0, 0, 0, 1), (1, 1, 1, 1, S3), (2, 0, 2, 1 + S3, S5)):
                        done = nc.tensor.matmul(ps[bank][:, 2 * W * lo:2 * W * (lo + n_)], wup[rows, k, :],
                                                nx[par][rows, 2 * W * a:2 * W * (a + n_)], start=True, stop=True)
                    done.then_inc(s["up_ps"], 1)
                return run

            def n1(t, par, gates=3):
                pe.wait_ge(s["red_sb"], 2 * t + 2)
                pe.wait_ge(s["n1_read"], t + 1)
                pe.wait_ge(s["g_read"], t + 4 - gates)
                for k in range(3):
                    done = nc.tensor.matmul(ps[3][:, 0:D], node[par][:, k, :, :, :].rearrange("p q h w -> p (q h w)"),
                                            wn1[:, k, :], start=(k == 0), stop=(k == 2))
                done.then_inc(s["n1_ps"], 1)

            def turn_h(t, par):
                pe.wait_ge(s["sil_out"], t + 1 + 2)
                pe.wait_ge(s["tx_sb"], t + 1)
                turn(hs[par], 5).then_inc(s["th_ps"], 1)

            def n2(t, par):
                pe.wait_ge(s["th_sb"], t + 1 + 1)
                pe.wait_ge(s["y_read"], t + 1)
                for k in range(2):
                    done = nc.tensor.matmul(ps[4][:, 0:D], ht[par][:, k, :], wn2[:, k, :], start=(k == 0), stop=(k == 1))
                done.then_inc(s["y_ps"], 1)

            def hidden(out_, a, lo):
                for m in range(HALF):
                    for k in range(2):
                        done = nc.tensor.matmul(out_[:, m * L:(m + 1) * L], w1_sb[:, k, (lo + m) * L:(lo + m + 1) * L],
                                                a[:, k, :], start=(k == 0), stop=(k == 1))
                return done

            def turn_x(t, par):
                pe.wait_ge(s["xf_ready"], t + 1)
                pe.wait_ge(s["th_sb"], t + 1 + 1)
                turn(xf[par], 5).then_inc(s["tx_ps"], 1)

            def lift(h):
                def run(t, par):
                    pe.wait_ge(s["tx_sb"], t + 1 + 1)
                    pe.wait_ge(s["h_sb"], 2 * t + h + 1)
                    hidden(ps[6 + h], hx[par], h * HALF).then_inc(s["h_ps"], 1)
                return run

            def gate(t, par, ahead=2):
                pe.wait_ge(s["h_sb"], 2 * t + 2 + 2)
                pe.wait_ge(s["n1_read"], (min(t + ahead, NT - 1) if isinstance(t, int) else t + ahead) + 1 + 1)
                pe.wait_ge(s["g_read"], t + 3)
                for m in range(HID // L):
                    done = nc.tensor.matmul(ps[3][:, 0:NE], hh[0][:, m, :], wgs[:, m, :], start=(m == 0), stop=(m == HID // L - 1))
                done.then_inc(s["g_ps"], 1)

            def fused():
                stages(pe, sums, (((1, up(0)), (2, turn_h), (3, lift(0))), ((1, up(1)), (2, n2)),
                                  ((1, n1), (3, lift(1))), ((2, turn_x), (3, gate))))

            def spill_sums(c, q):
                n_ = c * PAIRS + q
                pe.wait_ge(s["sp_in"], n_ + 1)
                for h in range(2):
                    done = nc.tensor.matmul(ps[0][h * P:(h + 1) * P, 0:BW], sp_pair, sp_ohs[h].rearrange("p k w -> p (k w)"), start=True, stop=True)
                done.then_inc(s["sp_ps"], 1)

            def apart():
                buckets(pe, sums)
                with pe.Fori(0, TILES) as c:
                    with pe.Fori(0, PAIRS) as q:
                        spill_sums(c, q)

                def tile(t, par):
                    up(0)(t, par)
                    up(1)(t, par)
                    n1(t, par, gates=1)
                    turn_h(t, par)
                    n2(t, par)
                    turn_x(t, par)
                    lift(0)(t, par)
                    lift(1)(t, par)
                    gate(t, par, ahead=0)

                tiles(pe, NT, tile)

            choose(pe, fused, apart)
            pe.wait_ge(s["ld_late"], 16 * (1 + NE))

            pe.wait_ge(s["ohx_ready"], 1)
            cells = (NE + 1) * NT
            flat = ohx[:, :, :].rearrange("p e t -> p (e t)")
            nc.tensor.matmul(ps[6][:, 0:cells], lowf[:, :], flat, start=True, stop=True)
            nc.tensor.matmul(ps[7][:, 0:cells], onesf[:, :], flat, start=True, stop=True).then_inc(s["rk_ps"], 1)

            def lift_m(i, j):
                par, t = j % 2, i * 4 + j
                pe.wait_ge(ld_mr[j % 4], (i + j // 4) * 16 + 16)
                pe.wait_ge(s["mt_sb"], t + 1)
                turn(mr[j % 4], par).then_inc(s["mt_ps"], 1)
                pe.wait_ge(s["mt_sb"], t + 1 + 2)
                pe.wait_ge(s["mh_sb"], t + 1)
                hidden(ps[2 + 2 * par], ht[par], 0)
                hidden(ps[3 + 2 * par], ht[par], HALF).then_inc(s["mh_ps"], 1)

            def expert(i, j, ex):
                par, t = j % 2, i * 4 + j
                pe.wait_ge(s["mh_sb"], t + 1 + 2)
                pe.wait_ge(s["my_sb"], t + 1 + 2)
                nc.tensor.matmul(ps[6 + par][:, 0:D], onesf[0:1, :], bd_sb[:, bass.ds(ex * D, D)], start=True, stop=False)
                for m in range(HID // L):
                    done = nc.tensor.matmul(ps[6 + par][:, 0:D], hh2[par][:, m, :], wd_sb[:, bass.ds(ex * (HID // L * D) + m * D, D)],
                                            start=False, stop=(m == HID // L - 1))
                done.then_inc(s["my_ps"], 1)

            pe.wait_ge(s["moe_rdy"], 1)
            lift_m(0, 0)

            def turn_m(i, last):
                ex = [pe.value_load(kei[0:1, bass.ds(i * 4 + j, 1)], min_val=0, max_val=NE - 1) for j in range(4)]
                for j in range(4):
                    if not (last and j == 3):
                        lift_m(i, j + 1)
                    expert(i, j, ex[j])

            with pe.Fori(0, MSLOTS // 4 - 1) as i:
                turn_m(i, False)
            turn_m(MSLOTS // 4 - 1, True)

        @block.vector
        def _(dve):
            v = s["v"]
            count = 0

            def own():
                nonlocal count
                count += 1
                return count

            dve.memset(srci[:, COLS:TILES], NB * W)
            dve.memset(dsti[:, COLS:TILES], 0)
            dve.memset(facs[:, COLS:TILES], 0.0)
            dve.memset(sph3[:, COLS, :], 0.0)
            dve.memset(sph5[:, COLS, :], 0.0)
            dve.memset(res[:, NT - 1, :], 0.0)
            dve.memset(zeros[:, :], 0.0).then_inc(s["msets"], 1)
            dve.memset(onehot[:, 0:GRP, :], 0.0)
            dve.memset(onesb[:, :], 1.0)
            for n_, k in (("n1_read", 1), ("y_read", 1), ("g_read", 3), ("my_sb", 4), ("pair_ready", RING), ("ohs_ready", 2)):
                dve.sem_inc(s[n_], k)
            dve.wait_ge(s["consts"], 9)
            dve.tensor_copy(keys[:, :], keysf[:, :])
            dve.tensor_scalar(base4, keysf[0:1, :].unsqueeze(1).broadcast_to([1, GRP, NK]), float(CAP), None, ALU.mult)
            dve.tensor_copy(lowb[:, :], lowf[:, :])
            dve.tensor_scalar(uppb[:, :], lowf[:, :], -1.0, 1.0, ALU.mult, ALU.add).then_inc(s["base_ready"], 1)
            dve.wait_ge(s["ld_idx"], 32)
            dve.wait_ge(s["ld_tail"], 32)
            dve.tensor_copy(dstf, dsti).then_inc(v, 1)
            dve.wait_ge(v, own())
            dve.tensor_scalar(dsti, srci, W - 1, None, ALU.bitwise_and).then_inc(v, 1)
            dve.wait_ge(v, own())
            dve.tensor_scalar(srci, srci, W.bit_length() - 1, None, ALU.logical_shift_right).then_inc(v, 1)
            dve.wait_ge(v, own())
            dve.tensor_copy(locf, dsti)
            dve.tensor_copy(keyf, srci)
            dve.tensor_copy(keyb, srci).then_inc(s["msets"], 1)
            dve.wait_ge(s["msets"], 2)

            def guess(y, v_, var, sm, base):
                dve.tensor_scalar(v_, var, LN_EPS, None, ALU.add).then_inc(sm, 1)
                dve.wait_ge(sm, base + 1)
                dve.tensor_scalar(y.bitcast(I32), v_.bitcast(I32), 1, None, ALU.logical_shift_right).then_inc(sm, 1)
                dve.wait_ge(sm, base + 2)
                dve.tensor_scalar(y.bitcast(I32), y.bitcast(I32), -1.0, RSQRT, ALU.mult, ALU.add).then_inc(sm, 1)
                dve.wait_ge(sm, base + 3)

            def rsqrt(y, v_, a, var, sm, base):
                guess(y, v_, var, sm, base)
                for n_ in range(3):
                    dve.scalar_tensor_tensor(a, y, v_, y, ALU.mult, ALU.mult).then_inc(sm, 1)
                    dve.wait_ge(sm, base + 3 * n_ + 4)
                    dve.tensor_scalar(a, a, -0.5, 1.5, ALU.mult, ALU.add).then_inc(sm, 1)
                    dve.wait_ge(sm, base + 3 * n_ + 5)
                    dve.tensor_tensor(y, y, a, ALU.mult).then_inc(sm, 1)
                    dve.wait_ge(sm, base + 3 * n_ + 6)

            def moments(t, par, sm, base):
                wait_apart(dve, sm, base)
                dve.bn_aggr(mv[par][:, :], st[par][:, :]).then_inc(sm, 1)
                wait_apart(dve, sm, base + 1)
                dve.tensor_copy(mvs[:, bass.ds(t, 1), :], mv[par][:, :].unsqueeze(1)).then_inc(sm, 1)
                dve.wait_ge(sm, base + 2)

            dve.wait_ge(s["ld_x"], 32)
            first = count

            def stats(t, par):
                dve.bn_stats(st[par][:, :], res[:, bass.ds(t, 1), :].rearrange("p a d -> p (a d)")).then_inc(v, 1)
                moments(t, par, v, first + 3 * t + 1)

            tiles(dve, NT, stats)
            count += 3 * NT
            guess(rs[:, :], vv[:, :], mvs[:, :, 1], v, count)
            count += 3
            for _ in range(3):
                dve.tensor_tensor(ra[:, :], rs[:, :], rs[:, :], ALU.mult).then_inc(v, 1)
                dve.wait_ge(v, own())
                dve.tensor_tensor(ra[:, :], ra[:, :], vv[:, :], ALU.mult).then_inc(v, 1)
                dve.wait_ge(v, own())
                dve.tensor_scalar(ra[:, :], ra[:, :], -0.5, 1.5, ALU.mult, ALU.add).then_inc(v, 1)
                dve.wait_ge(v, own())
                dve.tensor_tensor(rs[:, :], rs[:, :], ra[:, :], ALU.mult).then_inc(v, 1)
                dve.wait_ge(v, own())

            def norm_x(t, par):
                dve.wait_ge(s["xn_read"], t + 1)
                dve.tensor_scalar(xn[par], res[:, bass.ds(t, 1), :].rearrange("p a d -> p (a d)"), mvs[:, bass.ds(t, 1), 0],
                                  rs[:, bass.ds(t, 1)], ALU.subtract, ALU.mult).then_inc(s["xn_ready"], 1)
                dve.wait_ge(s["xn_ready"], t + 1)
                row = res[:, bass.ds(t, 1), :].rearrange("p a d -> p (a d)")
                dve.tensor_tensor(row, row, xn[par], ALU.add).then_inc(v, 1)
                dve.wait_ge(v, first_r + t + 1)

            first_r = count
            tiles(dve, NT, norm_x)
            count += NT

            dve.sem_inc(s["rank_read"], 1)
            dve.wait_ge(s["ld_edge"], 16 * 6)
            dve.wait_ge(s["tbl_out"], 16)
            first_c = count

            def places(i, par, first=False):
                n_ = 2 * i + par
                c0 = i * (2 * CHUNK) + par * CHUNK
                if not first:
                    dve.wait_ge(scat[par], CHUNK * 16 * i)
                for at_, a, k in ((R_FAC + 1, sph3, S3), (R_FAC + 1 + S3, sph5, S5)):
                    done = dve.tensor_tensor(rec[par][:, :, at_:at_ + k], a[:, bass.ds(c0, CHUNK), :],
                                             facs[:, bass.ds(c0, CHUNK)].unsqueeze(2).broadcast_to([L, CHUNK, k]), ALU.mult)
                done.then_inc(s["flds_v"], 1)
                dve.tensor_tensor(onehot[:, bass.ds(c0 + GRP, CHUNK), :], keyb[:, bass.ds(c0, CHUNK)].unsqueeze(2).broadcast_to([L, CHUNK, NK]),
                                  keys[:, :].unsqueeze(1).broadcast_to([L, CHUNK, NK]), ALU.is_equal).then_inc(s["oh_ready"], 1)
                dve.wait_ge(s["oh_ready"], n_ + 1)
                for q in range(CHUNK // GRP):
                    dve.wait_ge(s["rank_done"], n_ * (CHUNK // GRP) + q + 1)
                    dve.tensor_tensor(prod[:, q * GRP:(q + 1) * GRP, :], ps[0][:, 0:GRP * NK].rearrange("p (t k) -> p t k", k=NK),
                                      onehot[:, bass.ds(c0 + GRP + q * GRP, GRP), :], ALU.mult).then_inc(s["rank_read"], 1)
                dve.wait_ge(s["rank_read"], (n_ + 1) * (CHUNK // GRP) + 1)
                k = first_c + 3 * n_
                dve.tensor_reduce(posf[:, :], prod, AX.X, ALU.add).then_inc(v, 1)
                dve.wait_ge(v, k + 1)
                dve.scalar_tensor_tensor(rnk[:, :], keyf[:, bass.ds(c0, CHUNK)], -float(CAP), posf[:, :], ALU.mult, ALU.add).then_inc(v, 1)
                dve.wait_ge(v, k + 2)
                dve.tensor_scalar(ovr[:, bass.ds(c0, CHUNK)], rnk[:, :], float(CAP), float(1 << 20), ALU.is_ge, ALU.mult).then_inc(v, 1)
                dve.wait_ge(v, k + 3)
                dve.tensor_tensor(posi[par][:, :], posf[:, :], ovr[:, bass.ds(c0, CHUNK)], ALU.add).then_inc(s["pos_ready"], 1)
                dve.wait_ge(s["pos_ready"], n_ + 1)

            places(0, 0, first=True)
            places(0, 1, first=True)
            dve.tensor_tensor(res[:, :, :], res[:, :, :], bn2[:, :].unsqueeze(1).broadcast_to([L, NT, D]), ALU.add)
            with dve.Fori(1, CHUNKS // 2) as i:
                places(i, 0)
                places(i, 1)
            count += 3 * CHUNKS

            dve.tensor_reduce(mxo[:, :], ovr[:, :], AX.X, ALU.max).then_inc(s["sum_in"], 1)
            dve.wait_ge(s["sum_ps"], 1)
            dve.tensor_scalar(spill[:, :], ps[7][0:1, 0:1], 0.0, None, ALU.is_gt).then_inc(s["spill_set"], 1)
            for par in range(2):
                dve.wait_ge(scat[par], CHUNK * 16 * (CHUNKS // 2))
            dve.memset(agg[:, PAIRS, :, :], 0.0)

            def hot(i, j):
                o, b = j % 2, i * RING + j
                dve.wait_ge(s["ohs_ready"], b + 1)
                dve.wait_ge(ld_ring[j], 16 * i + 16)
                dve.tensor_tensor(oh5[o], ring[j][:, :, R_LOC:R_LOC + 1].broadcast_to([L, SLOTS, W]),
                                  iota_w[:, :].unsqueeze(1).broadcast_to([L, SLOTS, W]), ALU.is_equal).then_inc(s["oh_w"], 1)
                dve.wait_ge(s["oh_w"], b + 1)
                dve.wait_ge(s["agg_ps"], b + 1)
                dve.tensor_tensor(ohs[o], oh5[o].unsqueeze(2).broadcast_to([L, SLOTS, PLANES, W]),
                                  ring[j][:, :, R_FAC:R_FAC + PLANES].unsqueeze(3).broadcast_to([L, SLOTS, PLANES, W]),
                                  ALU.mult).then_inc(s["ohs_ready"], 1)

            def pairs(i, j):
                if not isinstance(i, int) or i * RING + j + 1 < NB:
                    hot(i + (j + 1) // RING, (j + 1) % RING)
                x_ = j % XRING
                dve.wait_ge(gath[x_], SLOTS * 16 * (i * (RING // XRING) + j // XRING + 1))
                dve.tensor_tensor(pair[j % 2], xg[x_], ring[j][:, :, 0:P], ALU.mult).then_inc(s["pair_ready"], 1)

            def pairx(t, par):
                last = 4 * t + 4
                dve.wait_ge(s["agg_sb"], (min(last, NB) if isinstance(t, int) else last) + 2)
                dve.wait_ge(s["up_ps"], 2 * t + 2)
                dve.tensor_tensor(nx[par].rearrange("p (s q w) -> p q s w", s=PLANES, q=2), agg[:, bass.ds(2 * t, 2), :, :],
                                  xT[:, bass.ds(2 * t, 2), :].unsqueeze(2).broadcast_to([L, 2, PLANES, W]), ALU.mult).then_inc(s["nx_ready"], 1)

            def norms(h):
                def run(t, par):
                    dve.wait_ge(s["up_sb"], 2 * t + h + 1 + 2)
                    for k, a, n_ in ((1, 0, S3), (2, S3, S5)):
                        done = dve.tensor_reduce(node[par][:, k, :, h, :], sq[par][:, h, a:a + n_, :].rearrange("p s (q w) -> p q w s", q=2), AX.X, ALU.add)
                    done.then_inc(s["red_sb"], 1)
                return run

            def norm_h(t, par):
                sm, k = s["hn_v"], 16 * t
                dve.wait_ge(s["n1_ps"], t + 1 + 2)
                dve.wait_ge(s["sil_out"], t + 1)
                dve.tensor_tensor(u[par], ps[3][:, 0:D], bn1[:, :], ALU.add).then_inc(s["n1_read"], 1)
                dve.wait_ge(s["n1_read"], t + 1 + 1)
                dve.bn_stats(st[0][:, :], u[par]).then_inc(sm, 1)
                wait_apart(dve, sm, k + 1)
                dve.bn_aggr(mv[0][:, :], st[0][:, :]).then_inc(sm, 1)
                dve.wait_ge(sm, k + 2)
                rsqrt(r1[0][:, :], v1[0][:, :], a1[0][:, :], mv[0][:, 1:2], sm, k + 2)
                dve.tensor_scalar(u[par], u[par], mv[0][:, 0:1], r1[0][:, :], ALU.subtract, ALU.mult).then_inc(sm, 1)
                dve.wait_ge(sm, k + 15)
                dve.tensor_tensor(u[par], u[par], gam[:, :], ALU.mult).then_inc(sm, 1)
                dve.wait_ge(sm, k + 16)
                dve.tensor_tensor(u[par], u[par], bet[:, :], ALU.add).then_inc(s["sil_in"], 1)

            def norm_f(t, par):
                sm, k = s["y_v"], 14 * t
                dve.wait_ge(s["y_ps"], t + 1)
                row = res[:, bass.ds(t, 1), :].rearrange("p a d -> p (a d)")
                dve.tensor_tensor(row, row, ps[4][:, 0:D], ALU.add).then_inc(s["y_read"], 1)
                wait_apart(dve, s["y_read"], t + 1 + 1)
                dve.bn_stats(st[1][:, :], row).then_inc(sm, 1)
                wait_apart(dve, sm, k + 1)
                dve.bn_aggr(mv[1][:, :], st[1][:, :]).then_inc(sm, 1)
                dve.wait_ge(sm, k + 2)
                rsqrt(r1[1][:, :], v1[1][:, :], a1[1][:, :], mv[1][:, 1:2], sm, k + 2)
                dve.tensor_scalar(hid[:, bass.ds(t, 1), :].rearrange("p a d -> p (a d)"), row, mv[1][:, 0:1], r1[1][:, :], ALU.subtract, ALU.mult)
                dve.wait_ge(s["tx_ps"], t + 1)
                dve.tensor_scalar(xf[par], row, mv[1][:, 0:1], r1[1][:, :], ALU.subtract, ALU.mult).then_inc(s["xf_ready"], 1)
                dve.wait_ge(s["xf_ready"], t + 1)

            def take_g(t, par):
                dve.wait_ge(s["g_ps"], t + 1 + 1)
                dve.tensor_tensor(lg[:, bass.ds(t, 1), :], ps[3][:, 0:NE].unsqueeze(1), bgr[:, :].unsqueeze(1), ALU.add).then_inc(s["g_read"], 1)

            def fused():
                stages(dve, pairs, (((1, pairx), (4, take_g)), ((1, norms(0)),), ((1, norms(1)), (2, norm_f)), ((1, norm_h),)))

            def spill_tile(c):
                def col(a):
                    return a[:, bass.ds(c, 1)]

                dve.tensor_scalar(sp_idx[:, :], col(dstf), 1.0, None, ALU.mult).then_inc(s["sp_ix"], 1)
                dve.scalar_tensor_tensor(sp_fac[:, 0:1], col(ovr), 1.0 / (1 << 20), col(facs), ALU.mult, ALU.mult).then_inc(s["sp_v"], 1)
                dve.wait_ge(s["sp_v"], 3 * c + 1)
                dve.tensor_scalar(sp_fac[:, 1:1 + S3], sph3[:, bass.ds(c, 1), :].rearrange("p a s -> p (a s)"), sp_fac[:, 0:1], None, ALU.mult)
                dve.tensor_scalar(sp_fac[:, 1 + S3:PLANES], sph5[:, bass.ds(c, 1), :].rearrange("p a s -> p (a s)"), sp_fac[:, 0:1], None, ALU.mult)
                dve.tensor_scalar(sp_oh, iota_w[:, :], col(locf), None, ALU.is_equal).then_inc(s["sp_v"], 1)
                dve.wait_ge(s["sp_v"], 3 * c + 2)
                dve.wait_ge(s["sp_ld"], 16 * c + 16)
                dve.wait_ge(s["sp_gx"], 16 * c + 16)
                dve.tensor_tensor(sp_pair, sp_x, sp_rbf, ALU.mult).then_inc(s["sp_v"], 1)
                wait_apart(dve, s["sp_v"], 3 * c + 3)
                with dve.Fori(0, PAIRS) as q:
                    n_ = c * PAIRS + q
                    for h in range(2):
                        done = dve.tensor_tensor(sp_eq[h][:, :], col(keyf), keysf[:, bass.ds(2 * q + h, 1)], ALU.is_equal)
                    done.then_inc(s["sp_a"], 1)
                    dve.wait_ge(s["sp_a"], n_ + 1)
                    for h in range(2):
                        done = dve.tensor_scalar(sp_key[h], sp_oh, sp_eq[h][:, :], None, ALU.mult)
                    done.then_inc(s["sp_b"], 1)
                    dve.wait_ge(s["sp_b"], n_ + 1)
                    for h in range(2):
                        done = dve.tensor_tensor(sp_ohs[h], sp_key[h].unsqueeze(1).broadcast_to([L, PLANES, W]),
                                                 sp_fac.unsqueeze(2).broadcast_to([L, PLANES, W]), ALU.mult)
                    done.then_inc(s["sp_in"], 1)
                    dve.wait_ge(s["sp_ps"], n_ + 1)
                    row = agg[:, bass.ds(q, 1), :, :].rearrange("p q s w -> p (q s w)")
                    dve.tensor_tensor(row, row, ps[0][:, 0:BW], ALU.add).then_inc(s["sp_add"], 1)
                    dve.wait_ge(s["sp_add"], n_ + 1)

            def apart():
                buckets(dve, pairs)
                dve.wait_ge(s["agg_sb"], NB + 2)
                dve.wait_ge(s["pair_ready"], NB + RING)
                with dve.Fori(0, TILES) as c:
                    spill_tile(c)

                def tile(t, par):
                    for run in (pairx, norms(0), norms(1), norm_h, norm_f, take_g):
                        run(t, par)

                tiles(dve, NT, tile)

            hot(0, 0)
            choose(dve, fused, apart)
            dve.wait_ge(s["g_read"], NT + 3)
            dve.wait_ge(s["g_ps"], NT + 1)

            def wide(a, n_):
                return a.unsqueeze(2).broadcast_to([L, NT, n_])

            dve.memset(zer[:, :], 0.0)
            dve.tensor_reduce(m1[:, :], lg[:, :, :], AX.X, ALU.max).then_inc(v, 1)
            dve.wait_ge(v, own())
            dve.tensor_tensor(le[:, :, :], lg[:, :, :], wide(m1[:, :], NE), ALU.subtract).then_inc(s["ex_in"], 1)
            dve.wait_ge(s["ex_in"], 1)
            dve.tensor_tensor(lg[:, :, :], lg[:, :, :], wide(m1[:, :], NE), ALU.is_ge).then_inc(v, 1)
            dve.wait_ge(v, own())
            dve.scalar_tensor_tensor(lg[:, :, :], lg[:, :, :], -float(NE), e9[:, 0:NE].unsqueeze(1).broadcast_to([L, NT, NE]),
                                     ALU.mult, ALU.add).then_inc(v, 1)
            dve.wait_ge(v, own())
            dve.tensor_reduce(eix[:, :], lg[:, :, :], AX.X, ALU.min).then_inc(v, 1)
            dve.wait_ge(v, own())
            dve.tensor_scalar(eix[:, :], eix[:, :], float(NE), None, ALU.add).then_inc(v, 1)
            dve.tensor_scalar(pad[:, :], tok[:, :], float(N), None, ALU.is_ge).then_inc(v, 1)
            own()
            dve.wait_ge(v, own())
            dve.tensor_scalar(tix[:, :], eix[:, :], -1.0, float(NE), ALU.mult, ALU.add).then_inc(v, 1)
            dve.wait_ge(v, own())
            dve.tensor_tensor(tix[:, :], tix[:, :], pad[:, :], ALU.mult).then_inc(v, 1)
            dve.wait_ge(v, own())
            dve.tensor_tensor(eix[:, :], eix[:, :], tix[:, :], ALU.add).then_inc(v, 1)
            dve.wait_ge(v, own())
            keys3 = [L, NE + 1, NT]
            dve.tensor_tensor(ohx[:, :, :], eix[:, :].unsqueeze(1).broadcast_to(keys3), e9[:, :].unsqueeze(2).broadcast_to(keys3),
                              ALU.is_equal).then_inc(s["ohx_ready"], 1)
            dve.tensor_scalar(recs[:, :, 2 * D + 1], tok[:, :], -1.0, float(TAG), ALU.mult, ALU.add)
            dve.wait_ge(s["ex_out"], 1)
            dve.tensor_reduce(m1[:, :], le[:, :, :], AX.X, ALU.add).then_inc(v, 1)
            dve.wait_ge(v, own())
            dve.reciprocal(recs[:, :, 2 * D], m1[:, :])
            dve.wait_ge(s["rk_ps"], 1)
            cells = (NE + 1) * NT
            flat = cum[:, :, :].rearrange("p e t -> p (e t)")
            dve.tensor_tensor_scan(flat, ps[7][:, 0:cells], zer[:, :], 0.0, ALU.add, ALU.add).then_inc(v, 1)
            dve.wait_ge(v, own())
            dve.tensor_copy(cnt[:, :], cum[:, :, NT - 1]).then_inc(v, 1)
            dve.tensor_copy(off[:, 0:1], zer[:, 0:1]).then_inc(v, 1)
            own()
            dve.wait_ge(v, own())
            dve.tensor_copy(off[:, 1:NE + 1], cnt[:, 0:NE]).then_inc(v, 1)
            dve.wait_ge(v, own())
            dve.tensor_tensor(cnt[:, :], cnt[:, :], off[:, :], ALU.subtract).then_inc(v, 1)
            dve.wait_ge(v, own())
            dve.tensor_scalar(cni[:, :], cnt[:, :], float(L - 1), None, ALU.add).then_inc(v, 1)
            dve.wait_ge(v, own())
            dve.tensor_scalar(cni[:, :], cni[:, :], L.bit_length() - 1, None, ALU.logical_shift_right).then_inc(v, 1)
            dve.wait_ge(v, own())
            dve.tensor_copy(slf[:, :], cni[:, :]).then_inc(v, 1)
            dve.wait_ge(v, own())
            dve.tensor_tensor_scan(csl[:, :], slf[:, :], zer[:, 0:NE + 1], 0.0, ALU.add, ALU.add).then_inc(v, 1)
            dve.wait_ge(v, own())
            dve.tensor_tensor(slf[:, :], csl[:, :], slf[:, :], ALU.subtract).then_inc(v, 1)
            dve.wait_ge(v, own())
            dve.scalar_tensor_tensor(off[:, :], slf[:, :], float(L), off[:, :], ALU.mult, ALU.subtract).then_inc(v, 1)
            dve.wait_ge(v, own())
            dve.tensor_tensor(cum[:, :, :], cum[:, :, :], ps[7][:, 0:cells].rearrange("p (e t) -> p e t", t=NT), ALU.subtract).then_inc(v, 1)
            dve.wait_ge(v, own())
            dve.tensor_tensor(cum[:, :, :], cum[:, :, :], ps[6][:, 0:cells].rearrange("p (e t) -> p e t", t=NT), ALU.add).then_inc(v, 1)
            dve.wait_ge(v, own())
            dve.tensor_tensor(cum[:, :, :], cum[:, :, :], off[:, :].unsqueeze(2).broadcast_to(keys3), ALU.add).then_inc(v, 1)
            dve.wait_ge(v, own())
            dve.tensor_tensor(sel[:, :, :], cum[:, :, :], ohx[:, :, :], ALU.mult).then_inc(v, 1)
            dve.wait_ge(v, own())
            dve.tensor_reduce(mpos[:, :], sel[:, :, :].rearrange("p e t -> p t e"), AX.X, ALU.add).then_inc(v, 1)
            dve.wait_ge(v, own())
            kshape = [L, MSLOTS, NE]
            dve.tensor_tensor(kcm[:, :, :], csl[:, 0:NE].unsqueeze(1).broadcast_to(kshape), kio[:, :].unsqueeze(2).broadcast_to(kshape),
                              ALU.is_le).then_inc(v, 1)
            dve.wait_ge(v, own())
            dve.tensor_reduce(kex[:, :], kcm[:, :, :], AX.X, ALU.add).then_inc(v, 1)
            dve.wait_ge(v, own())
            dve.tensor_scalar(kei[:, :], kex[:, :], float(NE - 1), None, ALU.min)
            dve.tensor_copy(mpi[:, :], mpos[:, :]).then_inc(s["moe_rdy"], 1)

            def finish(i, first=False):
                for j in range(4):
                    t, par = i * 4 + j, j % 2
                    if not (first and j < 2):
                        dve.wait_ge(wr_y[par], 32 * i + 16 * (j // 2))
                    dve.wait_ge(ld_mr[j], 16 * i + 16)
                    dve.tensor_scalar(oix[j][:, :], mr[j][:, 2 * D + 1:2 * D + 2], -1.0, float(TAG), ALU.mult, ALU.add)
                    dve.wait_ge(s["my_ps"], t + 1 + 2)
                    dve.scalar_tensor_tensor(yo[par], ps[6 + par][:, 0:D], mr[j][:, 2 * D:2 * D + 1], mr[j][:, D:2 * D],
                                             ALU.mult, ALU.add).then_inc(s["my_sb"], 1)

            finish(0, first=True)
            with dve.Fori(1, MSLOTS // 4) as i:
                finish(i)


_INS = ["x", "src", "dst", "edge_attr3_5x1", "edge_attr3_3x1", "edge_attr_64", "edge_weight1",
        "L0_gnn_W_down", "L0_gnn_b_down", "L0_gnn_W_up0", "L0_gnn_b_up0", "L0_gnn_W_up1", "L0_gnn_W_uph",
        "L0_gnn_W_n1", "L0_gnn_b_n1", "L0_gnn_ln_g", "L0_gnn_ln_b", "L0_gnn_W_n2", "L0_gnn_b_n2",
        "L0_ffn_W1", "L0_ffn_b1", "L0_ffn_Wg", "L0_ffn_bg", "L0_ffn_Wd", "L0_ffn_bd"]


def kernel(**inputs):
    import numpy as _np
    import concourse.bacc as _bacc
    from concourse import mybir as _mybir
    from concourse.bass_utils import run_bass_kernel_spmd as _run

    nc = _bacc.Bacc("TRN2", target_bir_lowering=False, num_devices=1)
    arrays, args = {}, []
    for name in _INS:
        a = _np.ascontiguousarray(inputs[name])
        arrays[f"in_{name}"] = a
        args.append(nc.dram_tensor(f"in_{name}", a.shape, _mybir.dt.from_np(a.dtype), kind="ExternalInput").ap())
    args.append(nc.dram_tensor("out_x", (N, D), _mybir.dt.float32, kind="ExternalOutput").ap())
    gnn_moe(nc, *args)
    r = _run(nc, [arrays], core_ids=[0])
    return r.results[0]["out_x"]
```

```python
import concourse.bass as bass
from concourse import mybir
from contextlib import ExitStack

F32 = mybir.dt.float32
BF16 = mybir.dt.bfloat16
I32 = mybir.dt.int32
ALU = mybir.AluOpType
ACT = mybir.ActivationFunctionType
AX = mybir.AxisListType

N, D, P, E = 3125, 256, 64, 53125
HID, NE = 1024, 8
S3, S5 = 3, 5
PLANES = 1 + S3 + S5
LN_EPS = 1e-5
L = 128
NT = -(-N // L)
N_FULL = N // L * L
N_TAIL = N - N_FULL
W = 32
NB = -(-N // W)
NK = NB + 1
PAIRS = NB // 2
SLOTS = 5
CAP = SLOTS * L
COLS = E // L
E_TAIL = E - COLS * L
TILES = COLS + 1
CHUNK = 16
CHUNKS = TILES // CHUNK
GRP = 4
REC = P + PLANES + 2
R_FAC, R_DST, R_LOC = P, P + PLANES, P + PLANES + 1
ROWS = NB * CAP
MREC = 2 * D + 2
MSLOTS = (N - NE) // L + NE
MSURE = NT // 4 * 4
TAG = 4096
HALF = HID // L // 2
RING, XRING = 8, 8
AHEAD = 6
RSQRT = float(0x5f3759df)
ZREPS = 10
WORK = 10632
BW = PLANES * W


def gnn_moe(nc, x, src, dst, sph_b, sph_a, rbf, fac, w_down, b_down, w_up0, b_up0, w_up1, w_uph,
            w_n1, b_n1, ln_g, ln_b, w_n2, b_n2, w1, b1, wg, bg, wd, bd, out):
    ctx = ExitStack()
    with ctx:
        def sb(name, shape, dt=F32):
            return ctx.enter_context(nc.sbuf_tensor(name, shape, dt))

        def sem(name):
            return ctx.enter_context(nc.semaphore(name))

        table = nc.dram_tensor("pair_table", [NT * L, P], F32, kind="Internal").ap()
        srt = nc.dram_tensor("sorted_edges", [ROWS, REC], F32, kind="Internal").ap()
        msrt = nc.dram_tensor("sorted_tokens", [(MSLOTS + 1) * L, MREC], F32, kind="Internal").ap()

        recs = sb("recs", [L, NT, MREC])
        hid = recs[:, :, 0:D]
        res = recs[:, :, D:2 * D]
        arena = sb("arena", [L, 20920])
        work = sb("work", [L, WORK])
        onehot = arena[:, 0:(TILES + GRP) * NK // 2].bitcast(BF16).rearrange("p (t k) -> p t k", k=NK)
        zcols = ROWS * REC // L // ZREPS
        zeros = arena[:, TILES * NK // 2 - zcols:TILES * NK // 2]
        agg = arena[:, 0:(PAIRS + 1) * BW].rearrange("p (q s w) -> p q s w", s=PLANES, w=W)
        at = (PAIRS + 1) * BW
        ring = []
        for n in range(RING):
            ring.append(arena[:, at:at + SLOTS * REC].rearrange("p (s r) -> p s r", r=REC))
            at += SLOTS * REC
        xg = []
        for n in range(XRING):
            xg.append(arena[:, at:at + SLOTS * P].rearrange("p (s c) -> p s c", c=P))
            at += SLOTS * P
        pair = []
        for n in range(2):
            pair.append(arena[:, at:at + SLOTS * P].rearrange("p (s c) -> p s c", c=P))
            at += SLOTS * P
        oh5 = []
        for n in range(2):
            oh5.append(arena[:, at:at + SLOTS * W].rearrange("p (s w) -> p s w", w=W))
            at += SLOTS * W
        assert at <= 20920
        wd_sb = arena[:, 0:NE * HID // L * D]
        bd_sb = arena[:, NE * HID // L * D:(NE * HID // L + NE) * D]
        at = 0

        def take(n):
            nonlocal at
            at += n
            return work[:, at - n:at]

        sph3 = take(TILES * S3).rearrange("p (t s) -> p t s", s=S3)
        sph5 = take(TILES * S5).rearrange("p (t s) -> p t s", s=S5)
        facs = take(TILES)
        dstf = take(TILES)
        locf = take(TILES)
        keyf = take(TILES)
        srci = take(TILES).bitcast(I32)
        dsti = take(TILES).bitcast(I32)
        keyb = take(TILES // 2).bitcast(BF16)
        at_rec = at
        rec = [take(CHUNK * REC).rearrange("p (t r) -> p t r", r=REC) for _ in range(2)]
        prod = take(CHUNK * NK).rearrange("p (t k) -> p t k", k=NK)
        assert at <= WORK
        tab = hid[:, :, 0:P]
        xn, xnt = ([hid[:, 2 * n:2 * n + 2, L:D] for n in (k, k + 1)] for k in (0, 2))
        base4 = hid[0:1, 8:8 + GRP, L:L + NK]
        at = 0
        nx = [take(2 * BW) for _ in range(2)]
        sq = [take(2 * 8 * 2 * W).rearrange("p (h s n) -> p h s n", h=2, s=8) for _ in range(2)]
        at_node = at
        node = [take(3 * L).rearrange("p (k q h w) -> p k q h w", k=3, q=2, h=2) for _ in range(2)]
        u = [take(D) for _ in range(2)]
        xf = [take(D) for _ in range(2)]
        hs = [take(D) for _ in range(2)]
        ht = [take(D).rearrange("p (k n) -> p k n", k=2) for _ in range(2)]
        hx = [take(D).rearrange("p (k n) -> p k n", k=2) for _ in range(2)]
        hh = take(HID).rearrange("p (j n) -> p j n", j=HID // L)
        at_ohs = at
        assert at_ohs >= at_rec
        ohs = [take(SLOTS * BW).rearrange("p (s k w) -> p s k w", k=PLANES, w=W) for _ in range(2)]
        lg = take(NT * NE).rearrange("p (t e) -> p t e", e=NE)
        assert at <= WORK
        at = at_ohs
        mr = [take(MREC) for _ in range(4)]
        yo = [take(D) for _ in range(2)]
        assert at <= WORK - NT * NE
        at = 0
        le = take(NT * NE).rearrange("p (t e) -> p t e", e=NE)
        ohx, cum, sel = (take((NE + 1) * NT).rearrange("p (e t) -> p e t", t=NT) for _ in range(3))
        zer = take((NE + 1) * NT)
        kcm = take(MSLOTS * NE).rearrange("p (k e) -> p k e", e=NE)
        tix, eix, pad, mpos = (take(NT) for _ in range(4))
        cnt, slf, csl, off = (take(NE + 1) for _ in range(4))
        kex = take(MSLOTS)
        cni, kei, kused, mpi = (take(n).bitcast(I32) for n in (NE + 1, MSLOTS, MSLOTS, NT))
        assert at <= at_node
        hh2 = [hh, work[:, at:at + HID].rearrange("p (j n) -> p j n", j=HID // L)]
        assert at + HID <= at_node
        at = (PAIRS + 1) * BW

        def tail(n):
            nonlocal at
            at += n
            return arena[:, at - n:at]

        sp_rbf, sp_x, sp_pair = tail(P), tail(P), tail(P)
        sp_fac = tail(PLANES)
        sp_oh = tail(W)
        sp_key = [tail(W) for _ in range(2)]
        sp_ohs = [tail(BW).rearrange("p (k w) -> p k w", w=W) for _ in range(2)]

        zeros_m = sb("zeros_m", [L, MREC // 2])
        xT = sb("xT", [L, PAIRS + 1, W])
        ident = sb("ident", [L, L])
        onesf = sb("onesf", [L, L])
        lowf = sb("lowf", [L, L])
        lowb = sb("lowb", [L, L], BF16)
        uppb = sb("uppb", [L, L], BF16)
        onesb = sb("onesb", [L, L], BF16)
        keys = sb("keys", [L, NK], BF16)
        keysf = sb("keysf", [L, NK])
        iota_w = sb("iota_w", [L, W])
        wdn = sb("wdn", [L, 2, P])
        bdn_row = sb("bdn_row", [1, P])
        bdn_col = sb("bdn_col", [L, 1])
        wup = sb("wup", [L, 3, L])
        bup = sb("bup", [L, 1])
        wn1 = sb("wn1", [L, 3, D])
        bn1 = sb("bn1", [L, D])
        gam = sb("gam", [L, D])
        bet = sb("bet", [L, D])
        wn2 = sb("wn2", [L, 2, D])
        bn2 = sb("bn2", [L, D])
        b1c = sb("b1c", [L, HID // L])
        w1_sb = sb("w1_sb", [L, 2, HID])
        wgs = sb("wgs", [L, HID // L, NE])
        bgr = sb("bgr", [L, NE])
        st = [sb(f"st{n}", [L, 6]) for n in range(2)]
        mv = [sb(f"mv{n}", [L, 2]) for n in range(2)]
        mvs = sb("mvs", [L, NT, 2])
        vv = sb("vv", [L, NT])
        mv2 = sb("mv2", [L, 2, 2])
        v2, r2, a2 = (sb(name, [L, 2]) for name in ("v2", "r2", "a2"))
        mxo = sb("mxo", [L, 1])
        spill = sb("spill", [1, 1], I32)
        sp_eq = [sb(f"sp_eq{n}", [L, 1]) for n in range(2)]
        sp_idx = sb("sp_idx", [L, 1], I32)
        rs = sb("rs", [L, NT])
        ra = sb("ra", [L, NT])
        posf = sb("posf", [L, CHUNK])
        rnk = sb("rnk", [L, CHUNK])
        ovr = sb("ovr", [L, TILES])
        posi = [sb(f"posi{n}", [L, CHUNK], I32) for n in range(2)]
        gidx = [sb(f"gidx{n}", [L, SLOTS], I32) for n in range(RING)]
        m1 = sb("m1", [L, NT])
        tok = sb("tok", [L, NT])
        e9 = sb("e9", [L, NE + 1])
        kio = sb("kio", [L, MSLOTS])
        oix = [sb(f"oix{n}", [L, 1], I32) for n in range(4)]

        ps = [ctx.enter_context(nc.psum_tensor(f"bank{n}", [L, 512], F32)) for n in range(8)]

        names = """turns ld_idx ld_tail ld_x ld_edge ld_w ld_late zfill zfill_m zeros_set msets x_v place_v consts tbl_out v
            xn_ready xn_read xt_sb pr_ps pr_sb
            oh_ready rank_done rank_read base_ready flds_v flds_a pos_ready sum_in sum_ps spill_set
            g_ready oh_w pair_ready ohs_ready agg_ps agg_sb
            nx_ready up_ps up_sb red_sb n1_ps n1_read ln_v hid_v sil_in sil_out th_ps th_sb y_ps y_read
            xf_ready tx_ps tx_sb h_ps h_sb g_ps g_read
            ex_in ex_out ohx_ready rk_ps tok_rdy moe_rdy tok_out
            mt_ps mt_sb mh_ps mh_sb my_ps my_v my_sb
            sp_ld sp_ix sp_gx sp_v sp_in sp_ps sp_add sp_a sp_b""".split()
        s = {n: sem(n) for n in names}
        ld_rec = [sem(f"ld_rec{n}") for n in range(2)]
        scat = [sem(f"scat{n}") for n in range(2)]
        ld_ring = [sem(f"ld_ring{n}") for n in range(RING)]
        gath = [sem(f"gath{n}") for n in range(XRING)]
        ld_mr = [sem(f"ld_mr{n}") for n in range(4)]
        wr_y = [sem(f"wr_y{n}") for n in range(2)]

        def wait_apart(eng, sm, value):
            eng.wait_ge(sm, value)
            eng.sem_inc(s["turns"], 1)

        def main_cols(a):
            return a[0:COLS * L].rearrange("(p c) -> p c", p=L)

        def tiles(eng, n, body):
            with eng.Fori(0, n // 2) as i:
                body(2 * i, 0)
                body(2 * i + 1, 1)
            if n % 2:
                body(n - 1, 0)

        def buckets(eng, body):
            whole = (NB - AHEAD) // RING
            with eng.Fori(0, whole) as i:
                for j in range(RING):
                    body(i, j)
            for b in range(whole * RING, NB):
                body(b // RING, b % RING)

        def stages(eng, bucket, stage, ending):
            def step(i, half, part=4):
                loop = not isinstance(i, int)
                for q in range(part):
                    bucket(i, 4 * half + q)
                    for lag, run in stage[q]:
                        if loop or 0 <= 2 * i + half - lag < NT:
                            run(2 * i + half - lag, (half - lag) % 2)

            for n_ in range(4):
                step(n_ // 2, n_ % 2)
            with eng.Fori(2, (NB - AHEAD) // RING) as i:
                step(i, 0)
                step(i, 1)
            for n_ in range((NB - AHEAD) // RING * 2, NT - 1):
                step(n_ // 2, n_ % 2)
            step((NT - 1) // 2, (NT - 1) % 2, part=NB - 4 * (NT - 1))
            for run, t in ending:
                run(t, t % 2)

        def choose(eng, fused, apart):
            eng.wait_ge(s["spill_set"], 1)
            full = eng.value_load(spill[0:1, 0:1], min_val=0, max_val=1)
            with eng.If(full):
                apart()
            with eng.Else():
                fused()

        def last_tiles(eng):
            used = [eng.value_load(kused[0:1, k:k + 1], min_val=0, max_val=1) for k in range(MSURE, MSLOTS)]

            def where(k, body):
                if k < MSURE:
                    body()
                elif k < MSLOTS:
                    with eng.If(used[k - MSURE]):
                        body()
            return where

        block = ctx.enter_context(nc.Block())

        @block.sync
        def _(sp):
            sp.dma_start(srci[:, 0:COLS], main_cols(src)).then_inc(s["ld_idx"], 16)
            sp.dma_start(dsti[:, 0:COLS], main_cols(dst)).then_inc(s["ld_idx"], 16)
            sp.dma_start(res[:, 0:NT - 1, :], x[0:N_FULL, :].rearrange("(t p) d -> p t d", p=L)).then_inc(s["ld_x"], 16)
            sp.wait_ge(s["msets"], 1)
            sp.dma_start(srci[0:E_TAIL, COLS:TILES], src[COLS * L:E].unsqueeze(1)).then_inc(s["ld_tail"], 16)
            sp.dma_start(dsti[0:E_TAIL, COLS:TILES], dst[COLS * L:E].unsqueeze(1)).then_inc(s["ld_tail"], 16)
            sp.dma_start(res[0:N_TAIL, NT - 1, :], x[N_FULL:N, :]).then_inc(s["ld_x"], 16)
            sp.dma_start(facs[:, 0:COLS], fac[0:COLS * L, :].rearrange("(p c) a -> p (c a)", p=L)).then_inc(s["ld_edge"], 16)
            sp.dma_start(sph3[:, 0:COLS, :], sph_a[0:COLS * L].rearrange("(p c) s a -> p c (s a)", p=L)).then_inc(s["ld_edge"], 16)
            sp.dma_start(sph5[:, 0:COLS, :], sph_b[0:COLS * L].rearrange("(p c) s a -> p c (s a)", p=L)).then_inc(s["ld_edge"], 16)
            sp.dma_start(facs[0:E_TAIL, COLS:TILES], fac[COLS * L:E, :]).then_inc(s["ld_edge"], 16)
            sp.dma_start(sph3[0:E_TAIL, COLS, :], sph_a[COLS * L:E].rearrange("p s a -> p (s a)")).then_inc(s["ld_edge"], 16)
            sp.dma_start(sph5[0:E_TAIL, COLS, :], sph_b[COLS * L:E].rearrange("p s a -> p (s a)")).then_inc(s["ld_edge"], 16)

            def load_chunk(i, par, c0, first=False, last=False):
                if not first:
                    sp.wait_ge(scat[par], CHUNK * 16 * i)
                rows = rbf[0:COLS * L, :].rearrange("(p c) f -> p c f", p=L)
                sp.dma_start(rec[par][:, 0:CHUNK - 1, 0:P], rows[:, bass.ds(c0, CHUNK - 1), :]).then_inc(ld_rec[par], 16)
                if last:
                    sp.dma_start(rec[par][0:E_TAIL, CHUNK - 1, 0:P], rbf[COLS * L:E, :]).then_inc(ld_rec[par], 16)
                else:
                    sp.dma_start(rec[par][:, CHUNK - 1:CHUNK, 0:P], rows[:, bass.ds(c0 + CHUNK - 1, 1), :]).then_inc(ld_rec[par], 16)

            load_chunk(0, 0, 0, first=True)
            load_chunk(0, 1, CHUNK, first=True)
            with sp.Fori(1, CHUNKS // 2 - 1) as i:
                load_chunk(i, 0, i * (2 * CHUNK))
                load_chunk(i, 1, i * (2 * CHUNK) + CHUNK)
            end = CHUNKS // 2 - 1
            load_chunk(end, 0, end * 2 * CHUNK)
            load_chunk(end, 1, end * 2 * CHUNK + CHUNK, last=True)

            for par in range(2):
                sp.wait_ge(scat[par], CHUNK * 16 * (CHUNKS // 2))
            by_bucket = srt.rearrange("(b p s) r -> b p s r", b=NB, s=SLOTS)

            def load_bucket(i, j):
                sp.wait_ge(s["pair_ready"], i * RING + j + 1)
                sp.dma_start(ring[j], by_bucket[bass.ds(i * RING + j, 1), :, :, :].rearrange("b p s r -> (b p) s r")).then_inc(ld_ring[j], 16)

            def spill_rows(c, tail=False):
                if not (isinstance(c, int) and c == 0):
                    sp.wait_ge(s["sp_v"], 3 * c)
                if tail:
                    sp.dma_start(sp_rbf[0:E_TAIL, :], rbf[COLS * L:E, :]).then_inc(s["sp_ld"], 16)
                else:
                    rows = rbf[0:COLS * L, :].rearrange("(p c) f -> p c f", p=L)
                    sp.dma_start(sp_rbf, rows[:, bass.ds(c, 1), :].rearrange("p c f -> p (c f)")).then_inc(s["sp_ld"], 16)

            def apart():
                buckets(sp, load_bucket)
                sp.wait_ge(s["pair_ready"], NB + RING)
                spill_rows(0)
                with sp.Fori(1, COLS) as c:
                    spill_rows(c)
                spill_rows(COLS, tail=True)

            choose(sp, lambda: buckets(sp, load_bucket), apart)
            sp.wait_ge(s["pair_ready"], NB + RING)
            sp.wait_ge(s["nx_ready"], NT)
            sp.dma_start(bd_sb, bd.rearrange("(a e) d -> a (e d)", a=1).broadcast_to([L, NE * D])).then_inc(s["ld_late"], 16)
            for e in range(NE):
                sp.dma_start(wd_sb.rearrange("p (e j d) -> p e j d", e=NE, j=HID // L)[:, e, :, :],
                             wd[e, :, :].rearrange("(j p) d -> p j d", p=L)).then_inc(s["ld_late"], 16)
            sp.wait_ge(s["tok_out"], 16 * NT)

            def load_tile(i, j):
                sp.wait_ge(s["my_sb"], i * 4 + j + 1)
                sp.dma_start(mr[j][:, :], msrt[bass.ds((i * 4 + j) * L, L), :]).then_inc(ld_mr[j], 16)

            with sp.Fori(0, MSURE // 4) as i:
                for j in range(4):
                    load_tile(i, j)
            sp.wait_ge(s["moe_rdy"], 1)
            where = last_tiles(sp)
            for k in range(MSURE, MSLOTS):
                where(k, lambda: load_tile(k // 4, k % 4))

        @block.gpsimd
        def _(gp):
            gp.iota(keysf[:, :], pattern=[[1, NK]], base=0, channel_multiplier=0, allow_small_or_imprecise_dtypes=True).then_inc(s["consts"], 1)
            gp.iota(iota_w[:, :], pattern=[[1, W]], base=0, channel_multiplier=0, allow_small_or_imprecise_dtypes=True).then_inc(s["consts"], 1)
            gp.iota(e9[:, :], pattern=[[1, NE + 1]], base=0, channel_multiplier=0, allow_small_or_imprecise_dtypes=True).then_inc(s["consts"], 1)
            gp.iota(kio[:, :], pattern=[[1, MSLOTS]], base=0, channel_multiplier=0, allow_small_or_imprecise_dtypes=True).then_inc(s["consts"], 1)
            gp.iota(tok[:, :], pattern=[[L, NT]], base=0, channel_multiplier=1, allow_small_or_imprecise_dtypes=True).then_inc(s["consts"], 1)
            gp.memset(onesf[:, :], 1.0).then_inc(s["consts"], 1)
            gp.memset(ident[:, :], 0.0).then_inc(s["consts"], 1)
            gp.wait_ge(s["consts"], 7)
            gp.affine_select(out=ident[:, :], in_=ident[:, :], compare_op=ALU.not_equal, fill=1.0, base=0,
                             pattern=[[-1, L]], channel_multiplier=1).then_inc(s["consts"], 1)
            gp.affine_select(out=lowf[:, :], in_=onesf[:, :], compare_op=ALU.is_gt, fill=0.0, base=0,
                             pattern=[[1, L]], channel_multiplier=-1).then_inc(s["consts"], 1)
            gp.wait_ge(s["consts"], 9)
            gp.wait_ge(s["zfill"], 16)

            def scatter_chunk(i, par):
                wait_apart(gp, ld_rec[par], 32 * (i + 1))
                wait_apart(gp, s["flds_v"], 2 * i + par + 1)
                wait_apart(gp, s["flds_a"], 2 * i + par + 1)
                wait_apart(gp, s["pos_ready"], 2 * i + par + 1)
                for c in range(CHUNK):
                    gp.indirect_dma_start(out=srt[:, :], out_offset=bass.IndirectOffsetOnAxis(ap=posi[par][:, c:c + 1], axis=0),
                                          in_=rec[par][:, c, :], in_offset=None, bounds_check=ROWS - 1,
                                          oob_is_err=False).then_inc(scat[par], 16)

            with gp.Fori(0, CHUNKS // 2) as i:
                scatter_chunk(i, 0)
                scatter_chunk(i, 1)
            def gather(i, j):
                x_ = j % XRING
                wait_apart(gp, s["g_ready"], i * RING + j + 1)
                wait_apart(gp, s["pair_ready"], i * RING + j + 1 + RING - XRING)
                for c in range(SLOTS):
                    gp.indirect_dma_start(out=xg[x_][:, c, :], out_offset=None, in_=table[:, :],
                                          in_offset=bass.IndirectOffsetOnAxis(ap=gidx[j][:, c:c + 1], axis=0)).then_inc(gath[x_], 16)

            def spill_gather(c):
                wait_apart(gp, s["sp_ix"], c + 1)
                gp.indirect_dma_start(out=sp_x, out_offset=None, in_=table[:, :],
                                      in_offset=bass.IndirectOffsetOnAxis(ap=sp_idx[:, 0:1], axis=0)).then_inc(s["sp_gx"], 16)

            def apart():
                buckets(gp, gather)
                with gp.Fori(0, TILES) as c:
                    spill_gather(c)

            gp.wait_ge(s["tbl_out"], 16)
            choose(gp, lambda: buckets(gp, gather), apart)
            gp.wait_ge(s["zfill_m"], 16)
            gp.wait_ge(s["tok_rdy"], 1)
            for t in range(NT):
                gp.indirect_dma_start(out=msrt[:, :], out_offset=bass.IndirectOffsetOnAxis(ap=mpi[:, t:t + 1], axis=0),
                                      in_=recs[:, t, :], in_offset=None).then_inc(s["tok_out"], 16)
            def write_rows(i, j):
                wait_apart(gp, s["my_sb"], i * 4 + j + 1 + 4)
                gp.indirect_dma_start(out=out[:, :], out_offset=bass.IndirectOffsetOnAxis(ap=oix[j][:, 0:1], axis=0),
                                      in_=yo[j % 2][:, :], in_offset=None, bounds_check=N - 1,
                                      oob_is_err=False).then_inc(wr_y[j % 2], 16)

            with gp.Fori(0, MSURE // 4) as i:
                for j in range(4):
                    write_rows(i, j)
            for par in range(2):
                gp.wait_ge(wr_y[par], 16 * MSURE // 2)
            gp.wait_ge(s["moe_rdy"], 1)
            where = last_tiles(gp)

            def write_last(k):
                write_rows(k // 4, k % 4)
                gp.wait_ge(wr_y[k % 2], 16 * (k // 2 + 1))

            for k in range(MSURE, MSLOTS):
                where(k, lambda: write_last(k))

        @block.scalar
        def _(act):
            loads = [(wdn[:, :, :], w_down.rearrange("(k p) c -> p k c", p=L)),
                     (bdn_row[:, :], b_down.unsqueeze(0)),
                     (bdn_col[0:P, :], b_down.unsqueeze(1)), (bdn_col[P:L, :], b_down.unsqueeze(1)),
                     (bup[:, :], b_up0.unsqueeze(1)),
                     (wn1[:, :, :], w_n1.rearrange("(k p) c -> p k c", p=L)), (bn1[:, :], b_n1.unsqueeze(0).broadcast_to([L, D])),
                     (gam[:, :], ln_g.unsqueeze(0).broadcast_to([L, D])), (bet[:, :], ln_b.unsqueeze(0).broadcast_to([L, D])),
                     (wn2[:, :, :], w_n2.rearrange("(k p) c -> p k c", p=L)), (bn2[:, :], b_n2.unsqueeze(0).broadcast_to([L, D])),
                     (wgs[:, :, :], wg.rearrange("(j p) e -> p j e", p=L)), (bgr[:, :], bg.unsqueeze(0).broadcast_to([L, NE]))]
            for h in range(2):
                for k, m in enumerate((w_up0, w_up1, w_uph)):
                    loads.append((wup[h * P:(h + 1) * P, k, :], m))
            act.wait_ge(s["zeros_set"], 1)
            act.wait_ge(s["ld_x"], 32)
            act.dma_start(srt.rearrange("(p a) r -> p (a r)", p=L).rearrange("p (n c) -> p n c", c=zcols),
                          zeros.unsqueeze(1).broadcast_to([L, ZREPS, zcols])).then_inc(s["zfill"], 16)
            for o, a in loads:
                act.dma_start(o, a).then_inc(s["ld_w"], 16)
            act.dma_start(b1c[:, :], b1.rearrange("(j p) -> p j", p=L), allow_slow_non_contiguous=True).then_inc(s["ld_w"], 16)
            act.dma_start(w1_sb[:, :, :], w1.rearrange("(k p) h -> p k h", p=L)).then_inc(s["ld_w"], 16)

            for n_, k in (("xt_sb", 1), ("pr_sb", 1), ("agg_sb", 2), ("up_sb", 2), ("sil_out", 2), ("th_sb", 1), ("tx_sb", 1),
                          ("h_sb", 2), ("mt_sb", 2), ("mh_sb", 2)):
                act.sem_inc(s[n_], k)

            def proj(t, par):
                act.wait_ge(s["xn_read"], t + 1 + 2)
                act.activation(xnt[par], ps[1][:, 0:D].rearrange("p (k n) -> p k n", k=2), ACT.Copy).then_inc(s["xt_sb"], 1)
                act.wait_ge(s["pr_ps"], t + 1)
                act.activation(tab[:, bass.ds(t, 1), :], ps[2][:, 0:P].unsqueeze(1), ACT.Copy)
                for h in range(2):
                    rows = slice(h * P, (h + 1) * P)
                    done = act.activation(xT[rows, bass.ds(2 * t, 2), :],
                                          ps[3 + h][rows, 0:2 * W].rearrange("p (q w) -> p q w", q=2),
                                          ACT.Identity, bias=bdn_col[rows, :])
                done.then_inc(s["pr_sb"], 1)

            def fields(i, par, first=False):
                c0 = i * (2 * CHUNK) + par * CHUNK
                if not first:
                    act.wait_ge(scat[par], CHUNK * 16 * i)
                for at_, a in ((R_FAC, facs), (R_DST, dstf), (R_LOC, locf)):
                    done = act.activation(rec[par][:, :, at_:at_ + 1], a[:, bass.ds(c0, CHUNK)].unsqueeze(2), ACT.Copy)
                done.then_inc(s["flds_a"], 1)

            act.wait_ge(s["msets"], 2)
            act.wait_ge(s["ld_edge"], 16 * 6)
            fields(0, 0, first=True)
            fields(0, 1, first=True)
            act.wait_ge(s["ld_w"], 16 * (len(loads) + 2))
            with act.Fori(1, CHUNKS // 2) as i:
                for par in range(2):
                    fields(i, par)
                    proj(2 * i - 2 + par, par)
            proj(NT - 1, 0)
            act.wait_ge(s["pr_sb"], NT + 1)
            act.dma_start(table.rearrange("(t p) c -> p t c", p=L), tab).then_inc(s["tbl_out"], 16)

            def indices(i, j):
                act.wait_ge(ld_ring[j], 16 * i + 16)
                act.wait_ge(s["pair_ready"], i * RING + j + 1)
                act.activation(gidx[j][:, :], ring[j][:, :, R_DST], ACT.Copy).then_inc(s["g_ready"], 1)

            def take_sums(i, j):
                ahead = j + AHEAD
                if not isinstance(i, int) or i * RING + ahead < NB:
                    indices(i + ahead // RING, ahead % RING)
                rows = slice(j % 2 * P, (j % 2 + 1) * P)
                act.wait_ge(s["agg_ps"], i * RING + j + 1 + 2)
                act.activation(agg[rows, bass.ds(i * (RING // 2) + j // 2, 1), :, :].rearrange("p q s w -> p (q s w)"),
                               ps[0][rows, 0:BW], ACT.Copy).then_inc(s["agg_sb"], 1)

            def squares(h):
                def run(t, par):
                    act.wait_ge(s["up_ps"], 2 * t + h + 1 + 4)
                    act.wait_ge(s["n1_ps"], t + 1)
                    act.activation(node[par][:, 0, :, h, :], ps[1][:, 0:2 * W].rearrange("p (q w) -> p q w", q=2),
                                   ACT.Identity, bias=bup[:, :])
                    act.activation(sq[par][:, h, 0:S3, :], ps[1][:, 2 * W:2 * W * (1 + S3)].rearrange("p (s n) -> p s n", s=S3), ACT.Square)
                    act.activation(sq[par][:, h, S3:S3 + S5, :], ps[2][:, 0:2 * W * S5].rearrange("p (s n) -> p s n", s=S5),
                                   ACT.Square).then_inc(s["up_sb"], 1)
                return run

            def silu(t, par):
                act.wait_ge(s["sil_in"], t + 1)
                act.wait_ge(s["th_ps"], t + 1)
                act.activation(hs[par], u[par], ACT.Silu).then_inc(s["sil_out"], 1)

            def turned_h(t, par):
                act.wait_ge(s["th_ps"], t + 1 + 2)
                act.activation(ht[par], ps[5][:, 0:D].rearrange("p (k n) -> p k n", k=2), ACT.Copy).then_inc(s["th_sb"], 1)

            def turned_x(t, par):
                act.wait_ge(s["tx_ps"], t + 1 + 2)
                act.activation(hx[par], ps[5][:, 0:D].rearrange("p (k n) -> p k n", k=2), ACT.Copy).then_inc(s["tx_sb"], 1)

            def gelus(bank, out_, lo):
                for m in range(HALF):
                    done = act.activation(out_[:, lo + m, :], ps[bank][:, m * L:(m + 1) * L], ACT.Gelu, bias=b1c[:, lo + m:lo + m + 1])
                return done

            def gelu(h):
                def run(t, par):
                    act.wait_ge(s["h_ps"], 2 * t + h + 1)
                    act.wait_ge(s["g_ps"], t + 1)
                    gelus(6 + h, hh, h * HALF).then_inc(s["h_sb"], 1)
                return run

            def fused():
                stages(act, take_sums, (((1, squares(0)), (3, turned_x)), ((1, squares(1)), (2, turned_h)),
                                        (), ((3, gelu(0)), (3, gelu(1)), (1, silu))),
                       [(squares(0), NT - 1), (squares(1), NT - 1), (gelu(0), NT - 4), (gelu(1), NT - 4), (silu, NT - 2),
                        (turned_x, NT - 3), (turned_h, NT - 2), (gelu(0), NT - 3), (gelu(1), NT - 3), (silu, NT - 1),
                        (turned_x, NT - 2), (turned_h, NT - 1), (gelu(0), NT - 2), (gelu(1), NT - 2),
                        (turned_x, NT - 1), (gelu(0), NT - 1), (gelu(1), NT - 1)])

            def apart():
                buckets(act, take_sums)
                act.wait_ge(s["sp_add"], TILES * PAIRS)

                def tile(t, par):
                    for run in (squares(0), squares(1), silu, turned_h, turned_x, gelu(0), gelu(1)):
                        run(t, par)

                tiles(act, NT, tile)

            for j in range(AHEAD):
                indices(0, j)
            act.dma_start(msrt.rearrange("(p a) r -> p (a r)", p=L).rearrange("p (n c) -> p n c", c=MREC // 2),
                          zeros_m[:, :].unsqueeze(1).broadcast_to([L, 2 * (MSLOTS + 1), MREC // 2])).then_inc(s["zfill_m"], 16)
            choose(act, fused, apart)
            act.wait_ge(s["ex_in"], 1)
            act.activation(le[:, :, :], le[:, :, :], ACT.Exp).then_inc(s["ex_out"], 1)

            def turned_m(t, par):
                act.wait_ge(s["mt_ps"], t + 1)
                act.activation(ht[par], ps[par][:, 0:D].rearrange("p (k n) -> p k n", k=2), ACT.Copy).then_inc(s["mt_sb"], 1)

            def gelu_m(t, par):
                act.wait_ge(s["mh_ps"], t + 1)
                act.wait_ge(s["my_ps"], t + 1)
                gelus(2 + 2 * par, hh2[par], 0)
                gelus(3 + 2 * par, hh2[par], HALF).then_inc(s["mh_sb"], 1)

            def both_m(t, par):
                gelu_m(t, par)
                turned_m(t + 1, 1 - par)

            turned_m(0, 0)
            tiles(act, MSURE - 2, both_m)
            where = last_tiles(act)
            for k in range(MSURE - 2, MSLOTS):
                where(k, lambda: gelu_m(k, k % 2))
                where(k + 1, lambda: turned_m(k + 1, (k + 1) % 2))

        @block.tensor
        def _(pe):
            for n_, k in (("xn_read", 2), ("agg_ps", 2), ("up_ps", 4), ("n1_ps", 2), ("th_ps", 2), ("tx_ps", 2), ("g_ps", 1), ("my_ps", 2)):
                pe.sem_inc(s[n_], k)
            pe.wait_ge(s["consts"], 9)

            def turn(src_, par):
                for k in range(2):
                    done = nc.tensor.transpose(ps[par][:, k * L:(k + 1) * L], src_[:, k * L:(k + 1) * L], ident[:, :])
                return done

            def proj(t, par):
                pe.wait_ge(s["xn_ready"], t + 1)
                pe.wait_ge(s["xt_sb"], t + 1)
                for k in range(2):
                    done = nc.tensor.transpose(ps[1][:, k * L:(k + 1) * L], xn[par][:, k, :], ident[:, :])
                done.then_inc(s["xn_read"], 1)
                pe.wait_ge(s["xt_sb"], t + 1 + 1)
                pe.wait_ge(s["pr_sb"], t + 1)
                for k in range(2):
                    nc.tensor.matmul(ps[2][:, 0:P], xnt[par][:, k, :], wdn[:, k, :], start=(k == 0), stop=False)
                nc.tensor.matmul(ps[2][:, 0:P], onesf[0:1, :], bdn_row[:, :], start=False, stop=True)
                for h in range(2):
                    for k in range(2):
                        done = nc.tensor.matmul(ps[3 + h][h * P:(h + 1) * P, 0:2 * W], wdn[:, k, :],
                                                xnt[par][:, k, :].rearrange("p (q h w) -> p h q w", q=2, h=2)[:, h, :, :],
                                                start=(k == 0), stop=(k == 1))
                done.then_inc(s["pr_ps"], 1)

            rank = ps[0][:, 0:GRP * NK]
            pe.wait_ge(s["base_ready"], 1)
            nc.tensor.matmul(rank, onesf[0:1, :], base4, start=True, stop=True)

            def ranks(i, par):
                for q in range(CHUNK // GRP):
                    g = i * (CHUNK // GRP) + q
                    if q == 0:
                        pe.wait_ge(s["oh_ready"], i + 1)
                    pe.wait_ge(s["rank_read"], g + 1)
                    for n_, m in ((0, uppb), (1, onesb), (2, onesb), (3, onesb), (4, lowb)):
                        done = nc.tensor.matmul(rank, m[:, :], onehot[:, bass.ds(g * GRP + n_, GRP), :].rearrange("p t k -> p (t k)"),
                                                start=False, stop=True, skip_group_check=True)
                    done.then_inc(s["rank_done"], 1)

            ranks(0, 0)
            ranks(1, 1)
            pe.wait_ge(s["ld_w"], 16 * 21)
            with pe.Fori(1, CHUNKS // 2) as i:
                for par in range(2):
                    ranks(2 * i + par, par)
                    proj(2 * i - 2 + par, par)
            proj(NT - 1, 0)

            pe.wait_ge(s["pr_sb"], NT + 1)
            pe.wait_ge(s["sum_in"], 1)
            nc.tensor.matmul(ps[7][:, 0:1], onesf[:, :], mxo[:, :], start=True, stop=True).then_inc(s["sum_ps"], 1)

            def sums(i, j):
                o, b = j % 2, i * RING + j
                pe.wait_ge(s["pair_ready"], b + 1 + RING)
                pe.wait_ge(s["ohs_ready"], b + 1 + 2)
                pe.wait_ge(s["agg_sb"], b + 1)
                for c in range(SLOTS):
                    done = nc.tensor.matmul(ps[0][o * P:(o + 1) * P, 0:BW], pair[o][:, c, :],
                                            ohs[o][:, c, :, :].rearrange("p k w -> p (k w)"), start=(c == 0), stop=(c == SLOTS - 1))
                done.then_inc(s["agg_ps"], 1)

            def up(h):
                def run(t, par):
                    pe.wait_ge(s["nx_ready"], t + 1)
                    pe.wait_ge(s["up_sb"], 2 * t + h + 2)
                    rows = slice(h * P, (h + 1) * P)
                    for bank, lo, k, a, n_ in ((1, 0, 0, 0, 1), (1, 1, 1, 1, S3), (2, 0, 2, 1 + S3, S5)):
                        done = nc.tensor.matmul(ps[bank][:, 2 * W * lo:2 * W * (lo + n_)], wup[rows, k, :],
                                                nx[par][rows, 2 * W * a:2 * W * (a + n_)], start=True, stop=True)
                    done.then_inc(s["up_ps"], 1)
                return run

            def n1(t, par, gates=3):
                pe.wait_ge(s["red_sb"], 2 * t + 2)
                pe.wait_ge(s["n1_read"], t + 1)
                pe.wait_ge(s["g_read"], t + 4 - gates)
                for k in range(3):
                    done = nc.tensor.matmul(ps[3][:, 0:D], node[par][:, k, :, :, :].rearrange("p q h w -> p (q h w)"),
                                            wn1[:, k, :], start=(k == 0), stop=(k == 2))
                done.then_inc(s["n1_ps"], 1)

            def turn_h(t, par):
                pe.wait_ge(s["sil_out"], t + 1 + 2)
                pe.wait_ge(s["tx_sb"], t + 1)
                turn(hs[par], 5).then_inc(s["th_ps"], 1)

            def n2(t, par):
                pe.wait_ge(s["th_sb"], t + 1 + 1)
                pe.wait_ge(s["y_read"], t + 1)
                for k in range(2):
                    done = nc.tensor.matmul(ps[4][:, 0:D], ht[par][:, k, :], wn2[:, k, :], start=(k == 0), stop=(k == 1))
                done.then_inc(s["y_ps"], 1)

            def hidden(out_, a, lo):
                for m in range(HALF):
                    for k in range(2):
                        done = nc.tensor.matmul(out_[:, m * L:(m + 1) * L], w1_sb[:, k, (lo + m) * L:(lo + m + 1) * L],
                                                a[:, k, :], start=(k == 0), stop=(k == 1))
                return done

            def turn_x(t, par):
                pe.wait_ge(s["xf_ready"], t + 1)
                pe.wait_ge(s["th_sb"], t + 1 + 1)
                turn(xf[par], 5).then_inc(s["tx_ps"], 1)

            def lift(h):
                def run(t, par):
                    pe.wait_ge(s["tx_sb"], t + 1 + 1)
                    pe.wait_ge(s["h_sb"], 2 * t + h + 1)
                    hidden(ps[6 + h], hx[par], h * HALF).then_inc(s["h_ps"], 1)
                return run

            def gate(t, par, ahead=2):
                pe.wait_ge(s["h_sb"], 2 * t + 2 + 2)
                pe.wait_ge(s["n1_read"], (min(t + ahead, NT - 1) if isinstance(t, int) else t + ahead) + 1 + 1)
                pe.wait_ge(s["g_read"], t + 3)
                for m in range(HID // L):
                    done = nc.tensor.matmul(ps[3][:, 0:NE], hh[:, m, :], wgs[:, m, :], start=(m == 0), stop=(m == HID // L - 1))
                done.then_inc(s["g_ps"], 1)

            def fused():
                stages(pe, sums, (((1, up(0)), (3, turn_x), (4, gate)), ((1, up(1)), (2, turn_h)),
                                  ((1, n1), (2, n2)), ((3, lift(0)), (3, lift(1)))),
                       [(n1, NT - 2), (n2, NT - 3), (up(0), NT - 1), (up(1), NT - 1), (lift(0), NT - 4), (lift(1), NT - 4),
                        (lambda t, par: n1(t, par, gates=4), NT - 1), (turn_x, NT - 3), (lambda t, par: gate(t, par, ahead=3), NT - 4),
                        (turn_h, NT - 2), (n2, NT - 2), (lift(0), NT - 3), (lift(1), NT - 3),
                        (turn_x, NT - 2), (gate, NT - 3), (turn_h, NT - 1), (n2, NT - 1), (lift(0), NT - 2), (lift(1), NT - 2),
                        (turn_x, NT - 1), (gate, NT - 2), (lift(0), NT - 1), (lift(1), NT - 1), (gate, NT - 1)])

            def spill_sums(c, q):
                n_ = c * PAIRS + q
                pe.wait_ge(s["sp_in"], n_ + 1)
                for h in range(2):
                    done = nc.tensor.matmul(ps[0][h * P:(h + 1) * P, 0:BW], sp_pair, sp_ohs[h].rearrange("p k w -> p (k w)"), start=True, stop=True)
                done.then_inc(s["sp_ps"], 1)

            def apart():
                buckets(pe, sums)
                with pe.Fori(0, TILES) as c:
                    with pe.Fori(0, PAIRS) as q:
                        spill_sums(c, q)

                def tile(t, par):
                    up(0)(t, par)
                    up(1)(t, par)
                    n1(t, par, gates=1)
                    turn_h(t, par)
                    n2(t, par)
                    turn_x(t, par)
                    lift(0)(t, par)
                    lift(1)(t, par)
                    gate(t, par, ahead=0)

                tiles(pe, NT, tile)

            choose(pe, fused, apart)
            pe.wait_ge(s["ld_late"], 16 * (1 + NE))

            pe.wait_ge(s["ohx_ready"], 1)
            cells = (NE + 1) * NT
            flat = ohx[:, :, :].rearrange("p e t -> p (e t)")
            nc.tensor.matmul(ps[6][:, 0:cells], lowf[:, :], flat, start=True, stop=True)
            nc.tensor.matmul(ps[7][:, 0:cells], onesf[:, :], flat, start=True, stop=True).then_inc(s["rk_ps"], 1)

            def turn_m(i, j):
                par, t = j % 2, i * 4 + j
                pe.wait_ge(ld_mr[j % 4], (i + j // 4) * 16 + 16)
                pe.wait_ge(s["mt_sb"], t + 1)
                turn(mr[j % 4], par).then_inc(s["mt_ps"], 1)

            def lift_m(i, j):
                par, t = j % 2, i * 4 + j
                pe.wait_ge(s["mt_sb"], t + 1 + 2)
                pe.wait_ge(s["mh_sb"], t + 1)
                hidden(ps[2 + 2 * par], ht[par], 0)
                hidden(ps[3 + 2 * par], ht[par], HALF).then_inc(s["mh_ps"], 1)

            def expert(i, j):
                par, t = j % 2, i * 4 + j
                ex = pe.value_load(kei[0:1, bass.ds(t, 1)], min_val=0, max_val=NE - 1)
                pe.wait_ge(s["mh_sb"], t + 1 + 2)
                pe.wait_ge(s["my_sb"], t + 1 + 2)
                for m in range(HID // L):
                    done = nc.tensor.matmul(ps[6 + par][:, 0:D], hh2[par][:, m, :], wd_sb[:, bass.ds(ex * (HID // L * D) + m * D, D)],
                                            start=(m == 0), stop=(m == HID // L - 1))
                done.then_inc(s["my_ps"], 1)

            pe.wait_ge(s["moe_rdy"], 1)
            turn_m(0, 0)
            lift_m(0, 0)
            turn_m(0, 1)
            with pe.Fori(0, MSURE // 4 - 1) as i:
                for j in range(4):
                    lift_m(i, j + 1)
                    turn_m(i, j + 2)
                    expert(i, j)
            where = last_tiles(pe)
            for k in range(MSURE - 4, MSLOTS):
                where(k + 1, lambda: lift_m(0, k + 1))
                where(k + 2, lambda: turn_m(0, k + 2))
                where(k, lambda: expert(0, k))

        @block.vector
        def _(dve):
            v = s["v"]
            count = 0

            def own():
                nonlocal count
                count += 1
                return count

            dve.memset(zeros, 0.0).then_inc(s["zeros_set"], 1)
            dve.memset(zeros_m[:, :], 0.0)
            dve.memset(srci[:, COLS:TILES], NB * W)
            dve.memset(dsti[:, COLS:TILES], 0)
            dve.memset(facs[:, COLS:TILES], 0.0)
            dve.memset(sph3[:, COLS, :], 0.0)
            dve.memset(sph5[:, COLS, :], 0.0)
            dve.memset(res[:, NT - 1, :], 0.0).then_inc(s["msets"], 1)
            dve.memset(onehot[:, 0:GRP, :], 0.0)
            dve.memset(onesb[:, :], 1.0)
            dve.memset(mv2[:, :, :], 0.0)
            for n_, k in (("n1_read", 1), ("y_read", 1), ("g_read", 3), ("my_sb", 4), ("pair_ready", RING), ("ohs_ready", 2)):
                dve.sem_inc(s[n_], k)
            dve.wait_ge(s["consts"], 9)
            dve.tensor_copy(keys[:, :], keysf[:, :])
            dve.tensor_scalar(base4, keysf[0:1, :].unsqueeze(1).broadcast_to([1, GRP, NK]), float(CAP), None, ALU.mult)
            dve.tensor_copy(lowb[:, :], lowf[:, :])
            dve.tensor_scalar(uppb[:, :], lowf[:, :], -1.0, 1.0, ALU.mult, ALU.add).then_inc(s["base_ready"], 1)
            dve.wait_ge(s["ld_idx"], 32)
            dve.wait_ge(s["ld_tail"], 32)
            dve.tensor_copy(dstf, dsti).then_inc(v, 1)
            dve.wait_ge(v, own())
            dve.tensor_scalar(dsti, srci, W - 1, None, ALU.bitwise_and).then_inc(v, 1)
            dve.wait_ge(v, own())
            dve.tensor_scalar(srci, srci, W.bit_length() - 1, None, ALU.logical_shift_right).then_inc(v, 1)
            dve.wait_ge(v, own())
            dve.tensor_copy(locf, dsti)
            dve.tensor_copy(keyf, srci)
            dve.tensor_copy(keyb, srci).then_inc(s["msets"], 1)
            dve.wait_ge(s["msets"], 2)

            def guess(y, v_, var, sm, base):
                dve.tensor_scalar(v_, var, LN_EPS, None, ALU.add).then_inc(sm, 1)
                dve.wait_ge(sm, base + 1)
                dve.tensor_scalar(y.bitcast(I32), v_.bitcast(I32), 1, None, ALU.logical_shift_right).then_inc(sm, 1)
                dve.wait_ge(sm, base + 2)
                dve.tensor_scalar(y.bitcast(I32), y.bitcast(I32), -1.0, RSQRT, ALU.mult, ALU.add).then_inc(sm, 1)
                dve.wait_ge(sm, base + 3)

            def rsqrt(y, v_, a, var, sm, base):
                guess(y, v_, var, sm, base)
                for n_ in range(3):
                    dve.tensor_tensor(a, y, y, ALU.mult).then_inc(sm, 1)
                    dve.wait_ge(sm, base + 3 * n_ + 4)
                    dve.scalar_tensor_tensor(a, a, -0.5, v_, ALU.mult, ALU.mult).then_inc(sm, 1)
                    dve.wait_ge(sm, base + 3 * n_ + 5)
                    dve.scalar_tensor_tensor(y, a, 1.5, y, ALU.add, ALU.mult).then_inc(sm, 1)
                    dve.wait_ge(sm, base + 3 * n_ + 6)

            def moments(t, par, sm, base):
                wait_apart(dve, sm, base)
                dve.bn_aggr(mv[par][:, :], st[par][:, :]).then_inc(sm, 1)
                wait_apart(dve, sm, base + 1)
                dve.tensor_copy(mvs[:, bass.ds(t, 1), :], mv[par][:, :].unsqueeze(1)).then_inc(sm, 1)
                dve.wait_ge(sm, base + 2)

            dve.wait_ge(s["ld_x"], 32)
            first = count

            def stats(t, par):
                dve.bn_stats(st[par][:, :], res[:, bass.ds(t, 1), :].rearrange("p a d -> p (a d)")).then_inc(v, 1)
                moments(t, par, v, first + 3 * t + 1)

            tiles(dve, NT, stats)
            count += 3 * NT
            rsqrt(rs[:, :], vv[:, :], ra[:, :], mvs[:, :, 1], v, count)
            count += 12

            dve.sem_inc(s["rank_read"], 1)
            dve.wait_ge(s["ld_edge"], 16 * 6)

            def one_hots(c0, q):
                cols = bass.ds(c0 + q * GRP, GRP)
                return dve.tensor_tensor(onehot[:, bass.ds(c0 + GRP + q * GRP, GRP), :], keyb[:, cols].unsqueeze(2).broadcast_to([L, GRP, NK]),
                                         keys[:, :].unsqueeze(1).broadcast_to([L, GRP, NK]), ALU.is_equal)

            def places(i, par, first=False, last=False):
                n_ = 2 * i + par
                c0 = i * (2 * CHUNK) + par * CHUNK
                dve.wait_ge(s["oh_ready"], n_ + 1)
                for q in range(CHUNK // GRP):
                    cols = slice(q * GRP, (q + 1) * GRP)
                    dve.wait_ge(s["rank_done"], n_ * (CHUNK // GRP) + q + 1)
                    dve.tensor_tensor(prod[:, cols, :], ps[0][:, 0:GRP * NK].rearrange("p (t k) -> p t k", k=NK),
                                      onehot[:, bass.ds(c0 + GRP + q * GRP, GRP), :], ALU.mult).then_inc(s["rank_read"], 1)
                    if not last:
                        done = one_hots(c0 + CHUNK, q)
                    dve.wait_ge(s["rank_read"], n_ * (CHUNK // GRP) + q + 2)
                    placed = dve.tensor_reduce(posf[:, cols], prod[:, cols, :], AX.X, ALU.add)
                if not last:
                    done.then_inc(s["oh_ready"], 1)
                placed.then_inc(s["place_v"], 1)
                k = 3 * n_
                dve.wait_ge(s["place_v"], k + 1)
                dve.scalar_tensor_tensor(rnk[:, :], keyf[:, bass.ds(c0, CHUNK)], -float(CAP), posf[:, :], ALU.mult, ALU.add).then_inc(s["place_v"], 1)
                dve.wait_ge(s["place_v"], k + 2)
                dve.tensor_scalar(ovr[:, bass.ds(c0, CHUNK)], rnk[:, :], float(CAP), float(1 << 20), ALU.is_ge, ALU.mult).then_inc(s["place_v"], 1)
                dve.wait_ge(s["place_v"], k + 3)
                if not first:
                    dve.wait_ge(scat[par], CHUNK * 16 * i)
                for at_, a, m in ((R_FAC + 1, sph3, S3), (R_FAC + 1 + S3, sph5, S5)):
                    done = dve.tensor_tensor(rec[par][:, :, at_:at_ + m], a[:, bass.ds(c0, CHUNK), :],
                                             facs[:, bass.ds(c0, CHUNK)].unsqueeze(2).broadcast_to([L, CHUNK, m]), ALU.mult)
                done.then_inc(s["flds_v"], 1)
                dve.tensor_tensor(posi[par][:, :], posf[:, :], ovr[:, bass.ds(c0, CHUNK)], ALU.add).then_inc(s["pos_ready"], 1)
                dve.wait_ge(s["pos_ready"], n_ + 1)

            for q in range(CHUNK // GRP):
                done = one_hots(0, q)
            done.then_inc(s["oh_ready"], 1)
            places(0, 0, first=True)
            places(0, 1, first=True)

            def norm_x(t, par):
                dve.wait_ge(s["xn_read"], t + 1)
                dve.tensor_scalar(xn[par], res[:, bass.ds(t, 1), :].rearrange("p a (k d) -> p (a k) d", k=2), mvs[:, bass.ds(t, 1), 0],
                                  rs[:, bass.ds(t, 1)], ALU.subtract, ALU.mult).then_inc(s["xn_ready"], 1)
                dve.wait_ge(s["xn_ready"], t + 1)
                row = res[:, bass.ds(t, 1), :].rearrange("p a (k d) -> p (a k) d", k=2)
                dve.tensor_tensor(row, row, xn[par], ALU.add).then_inc(s["x_v"], 1)
                dve.wait_ge(s["x_v"], t + 1)

            norm_x(0, 0)
            with dve.Fori(1, CHUNKS // 2 - 1) as i:
                for par in range(2):
                    places(i, par)
                    norm_x(2 * i - 1 + par, 1 - par)
            places(CHUNKS // 2 - 1, 0)
            norm_x(NT - 2, 1)
            places(CHUNKS // 2 - 1, 1, last=True)
            norm_x(NT - 1, 0)

            dve.tensor_reduce(mxo[:, :], ovr[:, :], AX.X, ALU.max).then_inc(s["sum_in"], 1)
            dve.tensor_tensor(res[:, :, :], res[:, :, :], bn2[:, :].unsqueeze(1).broadcast_to([L, NT, D]), ALU.add)
            dve.wait_ge(s["sum_ps"], 1)
            dve.tensor_scalar(spill[:, :], ps[7][0:1, 0:1], 0.0, None, ALU.is_gt).then_inc(s["spill_set"], 1)
            for par in range(2):
                dve.wait_ge(scat[par], CHUNK * 16 * (CHUNKS // 2))
            dve.memset(agg[:, PAIRS, :, :], 0.0)

            def hot(i, j):
                o, b = j % 2, i * RING + j
                dve.wait_ge(s["ohs_ready"], b + 1)
                dve.wait_ge(ld_ring[j], 16 * i + 16)
                dve.tensor_tensor(oh5[o], ring[j][:, :, R_LOC:R_LOC + 1].broadcast_to([L, SLOTS, W]),
                                  iota_w[:, :].unsqueeze(1).broadcast_to([L, SLOTS, W]), ALU.is_equal).then_inc(s["oh_w"], 1)
                dve.wait_ge(s["oh_w"], b + 1)
                dve.wait_ge(s["agg_ps"], b + 1)
                dve.tensor_tensor(ohs[o], oh5[o].unsqueeze(2).broadcast_to([L, SLOTS, PLANES, W]),
                                  ring[j][:, :, R_FAC:R_FAC + PLANES].unsqueeze(3).broadcast_to([L, SLOTS, PLANES, W]),
                                  ALU.mult).then_inc(s["ohs_ready"], 1)

            def pairs(i, j):
                x_ = j % XRING
                dve.wait_ge(gath[x_], SLOTS * 16 * (i * (RING // XRING) + j // XRING + 1))
                dve.tensor_tensor(pair[j % 2], xg[x_], ring[j][:, :, 0:P], ALU.mult).then_inc(s["pair_ready"], 1)
                if not isinstance(i, int) or i * RING + j + 1 < NB:
                    hot(i + (j + 1) // RING, (j + 1) % RING)

            def pairx(t, par):
                last = 4 * t + 4
                dve.wait_ge(s["agg_sb"], (min(last, NB) if isinstance(t, int) else last) + 2)
                dve.wait_ge(s["up_ps"], 2 * t + 2)
                dve.tensor_tensor(nx[par].rearrange("p (s q w) -> p q s w", s=PLANES, q=2), agg[:, bass.ds(2 * t, 2), :, :],
                                  xT[:, bass.ds(2 * t, 2), :].unsqueeze(2).broadcast_to([L, 2, PLANES, W]), ALU.mult).then_inc(s["nx_ready"], 1)

            def norms(h):
                def run(t, par):
                    dve.wait_ge(s["up_sb"], 2 * t + h + 1 + 2)
                    for k, a, n_ in ((1, 0, S3), (2, S3, S5)):
                        done = dve.tensor_reduce(node[par][:, k, :, h, :], sq[par][:, h, a:a + n_, :].rearrange("p s (q w) -> p q w s", q=2), AX.X, ALU.add)
                    done.then_inc(s["red_sb"], 1)
                return run

            def layer_norms(n_, h, f):
                sm, k = s["ln_v"], 17 * n_
                if h:
                    t, par = h
                    dve.wait_ge(s["n1_ps"], t + 1 + 2)
                    dve.wait_ge(s["sil_out"], t + 1)
                    dve.tensor_tensor(u[par], ps[3][:, 0:D], bn1[:, :], ALU.add).then_inc(s["n1_read"], 1)
                if f:
                    t, par = f
                    row = res[:, bass.ds(t, 1), :].rearrange("p a d -> p (a d)")
                    dve.wait_ge(s["y_ps"], t + 1)
                    dve.tensor_tensor(row, row, ps[4][:, 0:D], ALU.add).then_inc(s["y_read"], 1)
                if h:
                    t, par = h
                    dve.wait_ge(s["n1_read"], t + 1 + 1)
                    dve.bn_stats(st[0][:, :], u[par]).then_inc(sm, 1)
                if f:
                    t, par = f
                    wait_apart(dve, s["y_read"], t + 1 + 1)
                    dve.bn_stats(st[1][:, :], row).then_inc(sm, 1)
                if not (h and f):
                    dve.sem_inc(sm, 1)
                wait_apart(dve, sm, k + 2)
                if h:
                    dve.bn_aggr(mv2[:, 0, :], st[0][:, :]).then_inc(sm, 1)
                if f:
                    dve.bn_aggr(mv2[:, 1, :], st[1][:, :]).then_inc(sm, 1)
                if not (h and f):
                    dve.sem_inc(sm, 1)
                dve.wait_ge(sm, k + 4)
                if h:
                    t, par = h
                    dve.scalar_tensor_tensor(u[par], u[par], mv2[:, 0, 0:1], gam[:, :], ALU.subtract, ALU.mult).then_inc(sm, 1)
                else:
                    dve.sem_inc(sm, 1)
                rsqrt(r2[:, :], v2[:, :], a2[:, :], mv2[:, :, 1], sm, k + 5)
                if h:
                    t, par = h
                    dve.scalar_tensor_tensor(u[par], u[par], r2[:, 0:1], bet[:, :], ALU.mult, ALU.add).then_inc(s["sil_in"], 1)
                if f:
                    t, par = f
                    dve.wait_ge(s["tx_ps"], t + 1)
                    dve.tensor_scalar(xf[par], row, mv2[:, 1, 0:1], r2[:, 1:2], ALU.subtract, ALU.mult).then_inc(s["xf_ready"], 1)
                    dve.tensor_scalar(hid[:, bass.ds(t, 1), :].rearrange("p a d -> p (a d)"), row, mv2[:, 1, 0:1], r2[:, 1:2],
                                      ALU.subtract, ALU.mult).then_inc(s["hid_v"], 1)
                    dve.wait_ge(s["hid_v"], t + 1)
                if h:
                    dve.wait_ge(s["sil_in"], h[0] + 1)

            def norm(t, par):
                layer_norms(t, (t, par) if not isinstance(t, int) or t < NT else None,
                            (t - 1, 1 - par) if not isinstance(t, int) or t > 0 else None)

            def take_g(t, par):
                dve.wait_ge(s["g_ps"], t + 1 + 1)
                dve.tensor_tensor(lg[:, bass.ds(t, 1), :], ps[3][:, 0:NE].unsqueeze(1), bgr[:, :].unsqueeze(1), ALU.add).then_inc(s["g_read"], 1)

            def fused():
                stages(dve, pairs, (((1, pairx),), ((1, norms(0)), (4, take_g)), ((1, norms(1)),), ((1, norm),)),
                       [(norms(1), NT - 2), (pairx, NT - 1), (norm, NT - 2), (norms(0), NT - 1), (norms(1), NT - 1),
                        (norm, NT - 1), (take_g, NT - 4), (take_g, NT - 3), (norm, NT), (take_g, NT - 2), (take_g, NT - 1)])

            def spill_tile(c):
                def col(a):
                    return a[:, bass.ds(c, 1)]

                dve.tensor_scalar(sp_idx[:, :], col(dstf), 1.0, None, ALU.mult).then_inc(s["sp_ix"], 1)
                dve.scalar_tensor_tensor(sp_fac[:, 0:1], col(ovr), 1.0 / (1 << 20), col(facs), ALU.mult, ALU.mult).then_inc(s["sp_v"], 1)
                dve.wait_ge(s["sp_v"], 3 * c + 1)
                dve.tensor_scalar(sp_fac[:, 1:1 + S3], sph3[:, bass.ds(c, 1), :].rearrange("p a s -> p (a s)"), sp_fac[:, 0:1], None, ALU.mult)
                dve.tensor_scalar(sp_fac[:, 1 + S3:PLANES], sph5[:, bass.ds(c, 1), :].rearrange("p a s -> p (a s)"), sp_fac[:, 0:1], None, ALU.mult)
                dve.tensor_scalar(sp_oh, iota_w[:, :], col(locf), None, ALU.is_equal).then_inc(s["sp_v"], 1)
                dve.wait_ge(s["sp_v"], 3 * c + 2)
                dve.wait_ge(s["sp_ld"], 16 * c + 16)
                dve.wait_ge(s["sp_gx"], 16 * c + 16)
                dve.tensor_tensor(sp_pair, sp_x, sp_rbf, ALU.mult).then_inc(s["sp_v"], 1)
                wait_apart(dve, s["sp_v"], 3 * c + 3)
                with dve.Fori(0, PAIRS) as q:
                    n_ = c * PAIRS + q
                    for h in range(2):
                        done = dve.tensor_tensor(sp_eq[h][:, :], col(keyf), keysf[:, bass.ds(2 * q + h, 1)], ALU.is_equal)
                    done.then_inc(s["sp_a"], 1)
                    dve.wait_ge(s["sp_a"], n_ + 1)
                    for h in range(2):
                        done = dve.tensor_scalar(sp_key[h], sp_oh, sp_eq[h][:, :], None, ALU.mult)
                    done.then_inc(s["sp_b"], 1)
                    dve.wait_ge(s["sp_b"], n_ + 1)
                    for h in range(2):
                        done = dve.tensor_tensor(sp_ohs[h], sp_key[h].unsqueeze(1).broadcast_to([L, PLANES, W]),
                                                 sp_fac.unsqueeze(2).broadcast_to([L, PLANES, W]), ALU.mult)
                    done.then_inc(s["sp_in"], 1)
                    dve.wait_ge(s["sp_ps"], n_ + 1)
                    row = agg[:, bass.ds(q, 1), :, :].rearrange("p q s w -> p (q s w)")
                    dve.tensor_tensor(row, row, ps[0][:, 0:BW], ALU.add).then_inc(s["sp_add"], 1)
                    dve.wait_ge(s["sp_add"], n_ + 1)

            def apart():
                buckets(dve, pairs)
                dve.wait_ge(s["agg_sb"], NB + 2)
                dve.wait_ge(s["pair_ready"], NB + RING)
                with dve.Fori(0, TILES) as c:
                    spill_tile(c)

                def tile(t, par):
                    for run in (pairx, norms(0), norms(1)):
                        run(t, par)
                    layer_norms(2 * t, (t, par), None)
                    layer_norms(2 * t + 1, None, (t, par))
                    take_g(t, par)

                tiles(dve, NT, tile)

            hot(0, 0)
            choose(dve, fused, apart)
            dve.wait_ge(s["g_read"], NT + 3)
            dve.wait_ge(s["g_ps"], NT + 1)

            def wide(a, n_):
                return a.unsqueeze(2).broadcast_to([L, NT, n_])

            dve.memset(zer[:, :], 0.0)
            dve.tensor_reduce(m1[:, :], lg[:, :, :], AX.X, ALU.max).then_inc(v, 1)
            dve.wait_ge(v, own())
            dve.tensor_tensor(le[:, :, :], lg[:, :, :], wide(m1[:, :], NE), ALU.subtract).then_inc(s["ex_in"], 1)
            dve.wait_ge(s["ex_in"], 1)
            dve.tensor_tensor(lg[:, :, :], lg[:, :, :], wide(m1[:, :], NE), ALU.is_ge).then_inc(v, 1)
            dve.wait_ge(v, own())
            dve.scalar_tensor_tensor(lg[:, :, :], lg[:, :, :], -float(NE), e9[:, 0:NE].unsqueeze(1).broadcast_to([L, NT, NE]),
                                     ALU.mult, ALU.add).then_inc(v, 1)
            dve.wait_ge(v, own())
            dve.tensor_reduce(eix[:, :], lg[:, :, :], AX.X, ALU.min).then_inc(v, 1)
            dve.wait_ge(v, own())
            dve.tensor_scalar(eix[:, :], eix[:, :], float(NE), None, ALU.add).then_inc(v, 1)
            dve.tensor_scalar(pad[:, :], tok[:, :], float(N), None, ALU.is_ge).then_inc(v, 1)
            own()
            dve.wait_ge(v, own())
            dve.tensor_scalar(tix[:, :], eix[:, :], -1.0, float(NE), ALU.mult, ALU.add).then_inc(v, 1)
            dve.wait_ge(v, own())
            dve.tensor_tensor(tix[:, :], tix[:, :], pad[:, :], ALU.mult).then_inc(v, 1)
            dve.wait_ge(v, own())
            dve.tensor_tensor(eix[:, :], eix[:, :], tix[:, :], ALU.add).then_inc(v, 1)
            dve.wait_ge(v, own())
            keys3 = [L, NE + 1, NT]
            dve.tensor_tensor(ohx[:, :, :], eix[:, :].unsqueeze(1).broadcast_to(keys3), e9[:, :].unsqueeze(2).broadcast_to(keys3),
                              ALU.is_equal).then_inc(s["ohx_ready"], 1)
            dve.tensor_scalar(recs[:, :, 2 * D + 1], tok[:, :], -1.0, float(TAG), ALU.mult, ALU.add)
            dve.wait_ge(s["ex_out"], 1)
            dve.tensor_reduce(m1[:, :], le[:, :, :], AX.X, ALU.add).then_inc(v, 1)
            dve.wait_ge(v, own())
            dve.reciprocal(recs[:, :, 2 * D], m1[:, :])
            dve.wait_ge(s["rk_ps"], 1)
            cells = (NE + 1) * NT
            flat = cum[:, :, :].rearrange("p e t -> p (e t)")
            dve.tensor_tensor_scan(flat, ps[7][:, 0:cells], zer[:, :], 0.0, ALU.add, ALU.add).then_inc(v, 1)
            dve.wait_ge(v, own())
            dve.tensor_copy(cnt[:, :], cum[:, :, NT - 1]).then_inc(v, 1)
            dve.tensor_copy(off[:, 0:1], zer[:, 0:1]).then_inc(v, 1)
            own()
            dve.wait_ge(v, own())
            dve.tensor_copy(off[:, 1:NE + 1], cnt[:, 0:NE]).then_inc(v, 1)
            dve.wait_ge(v, own())
            dve.tensor_tensor(cnt[:, :], cnt[:, :], off[:, :], ALU.subtract).then_inc(v, 1)
            dve.wait_ge(v, own())
            dve.tensor_scalar(cni[:, :], cnt[:, :], float(L - 1), None, ALU.add).then_inc(v, 1)
            dve.wait_ge(v, own())
            dve.tensor_scalar(cni[:, :], cni[:, :], L.bit_length() - 1, None, ALU.logical_shift_right).then_inc(v, 1)
            dve.wait_ge(v, own())
            dve.tensor_copy(slf[:, :], cni[:, :]).then_inc(v, 1)
            dve.wait_ge(v, own())
            dve.tensor_tensor_scan(csl[:, :], slf[:, :], zer[:, 0:NE + 1], 0.0, ALU.add, ALU.add).then_inc(v, 1)
            dve.wait_ge(v, own())
            dve.tensor_tensor(slf[:, :], csl[:, :], slf[:, :], ALU.subtract).then_inc(v, 1)
            dve.wait_ge(v, own())
            dve.scalar_tensor_tensor(off[:, :], slf[:, :], float(L), off[:, :], ALU.mult, ALU.subtract).then_inc(v, 1)
            dve.wait_ge(v, own())
            dve.tensor_tensor(cum[:, :, :], cum[:, :, :], ps[7][:, 0:cells].rearrange("p (e t) -> p e t", t=NT), ALU.subtract).then_inc(v, 1)
            dve.wait_ge(v, own())
            dve.tensor_tensor(cum[:, :, :], cum[:, :, :], ps[6][:, 0:cells].rearrange("p (e t) -> p e t", t=NT), ALU.add).then_inc(v, 1)
            dve.wait_ge(v, own())
            dve.tensor_tensor(cum[:, :, :], cum[:, :, :], off[:, :].unsqueeze(2).broadcast_to(keys3), ALU.add).then_inc(v, 1)
            dve.wait_ge(v, own())
            dve.tensor_tensor(sel[:, :, :], cum[:, :, :], ohx[:, :, :], ALU.mult).then_inc(v, 1)
            dve.wait_ge(v, own())
            dve.tensor_reduce(mpos[:, :], sel[:, :, :].rearrange("p e t -> p t e"), AX.X, ALU.add).then_inc(v, 1)
            dve.wait_ge(v, own())
            dve.tensor_copy(mpi[:, :], mpos[:, :]).then_inc(s["tok_rdy"], 1)
            kshape = [L, MSLOTS, NE]
            dve.tensor_tensor(kcm[:, :, :], csl[:, 0:NE].unsqueeze(1).broadcast_to(kshape), kio[:, :].unsqueeze(2).broadcast_to(kshape),
                              ALU.is_le).then_inc(v, 1)
            dve.wait_ge(v, own())
            dve.tensor_reduce(kex[:, :], kcm[:, :, :], AX.X, ALU.add).then_inc(v, 1)
            dve.wait_ge(v, own())
            dve.tensor_scalar(kei[:, :], kex[:, :], float(NE - 1), None, ALU.min)
            dve.tensor_scalar(kused[:, :], kex[:, :], float(NE), None, ALU.is_lt).then_inc(s["moe_rdy"], 1)

            def finish(i, j, first=False):
                t, par = i * 4 + j, j % 2
                ex = dve.value_load(kei[0:1, bass.ds(t, 1)], min_val=0, max_val=NE - 1)
                if not (first and j < 2):
                    dve.wait_ge(wr_y[par], 32 * i + 16 * (j // 2))
                dve.wait_ge(ld_mr[j], 16 * i + 16)
                dve.tensor_scalar(oix[j][:, :], mr[j][:, 2 * D + 1:2 * D + 2], -1.0, float(TAG), ALU.mult, ALU.add)
                dve.wait_ge(s["my_ps"], t + 1 + 2)
                dve.tensor_tensor(yo[par], ps[6 + par][:, 0:D], bd_sb[:, bass.ds(ex * D, D)], ALU.add).then_inc(s["my_v"], 1)
                dve.wait_ge(s["my_v"], t + 1)
                dve.scalar_tensor_tensor(yo[par], yo[par], mr[j][:, 2 * D:2 * D + 1], mr[j][:, D:2 * D],
                                         ALU.mult, ALU.add).then_inc(s["my_sb"], 1)

            dve.wait_ge(s["ld_late"], 16 * (1 + NE))
            dve.wait_ge(s["moe_rdy"], 1)
            for j in range(4):
                finish(0, j, first=True)
            with dve.Fori(1, MSURE // 4) as i:
                for j in range(4):
                    finish(i, j)
            where = last_tiles(dve)
            for k in range(MSURE, MSLOTS):
                where(k, lambda: finish(k // 4, k % 4))


_INS = ["x", "src", "dst", "edge_attr3_5x1", "edge_attr3_3x1", "edge_attr_64", "edge_weight1",
        "L0_gnn_W_down", "L0_gnn_b_down", "L0_gnn_W_up0", "L0_gnn_b_up0", "L0_gnn_W_up1", "L0_gnn_W_uph",
        "L0_gnn_W_n1", "L0_gnn_b_n1", "L0_gnn_ln_g", "L0_gnn_ln_b", "L0_gnn_W_n2", "L0_gnn_b_n2",
        "L0_ffn_W1", "L0_ffn_b1", "L0_ffn_Wg", "L0_ffn_bg", "L0_ffn_Wd", "L0_ffn_bd"]


def kernel(**inputs):
    import numpy as _np
    import concourse.bacc as _bacc
    from concourse import mybir as _mybir
    from concourse.bass_utils import run_bass_kernel_spmd as _run

    nc = _bacc.Bacc("TRN2", target_bir_lowering=False, num_devices=1)
    arrays, args = {}, []
    for name in _INS:
        a = _np.ascontiguousarray(inputs[name])
        arrays[f"in_{name}"] = a
        args.append(nc.dram_tensor(f"in_{name}", a.shape, _mybir.dt.from_np(a.dtype), kind="ExternalInput").ap())
    args.append(nc.dram_tensor("out_x", (N, D), _mybir.dt.float32, kind="ExternalOutput").ap())
    gnn_moe(nc, *args)
    r = _run(nc, [arrays], core_ids=[0])
    return r.results[0]["out_x"]
```
